# Optimizing a Trainium2 kernel written in Bass

```python
import numpy as np
import jax
import jax.numpy as jnp

def _softmax(x, axis=-1):
    return jax.nn.softmax(x, axis=axis)

def _gelu(x):
    return jax.nn.gelu(x, approximate=True)

def _silu(x):
    return jax.nn.silu(x)

def _sigmoid(x):
    return jax.nn.sigmoid(x)

def _layernorm(x, axis=-1, eps=1e-05):
    m = jnp.mean(x, axis=axis, keepdims=True)
    v = jnp.var(x, axis=axis, keepdims=True)
    return (x - m) / jnp.sqrt(v + eps)

def _scatter_add(tgt, idx, src, axis=0):
    return tgt.at[idx].add(src)

def _segment_sum(src, seg, n):
    return jax.ops.segment_sum(src, seg, n)
kernel_name = 'mk_gnn_preln_d1_gnn_r64_70a215'

def setup_inputs(seed: int=0):
    np.random.seed(seed)
    _w = jnp.asarray

    def _rec_inputs():
        import jax
        import jax.numpy as jnp
        _gk = jax.random.key(seed)
        x = -0.000202 + 1 * jax.random.normal(jax.random.fold_in(_gk, 1), (100000, 64), jnp.float32)
        _s = jax.random.randint(jax.random.fold_in(_gk, 2), (25000,), 0, 100000, jnp.int32)
        _d = jax.random.randint(jax.random.fold_in(_gk, 3), (25000,), 0, 100000, jnp.int32)
        _loop = jnp.arange(100000, dtype=jnp.int32)
        src = jnp.concatenate([_s, _d, _loop])
        dst = jnp.concatenate([_d, _s, _loop])
        _o = jnp.argsort(dst, stable=True)
        src = src[_o]
        dst = dst[_o]
        return (x, src, dst)
    x, src, dst = _rec_inputs()

    def _L0_gnn_setup():
        import jax, jax.numpy as jnp
        import numpy as np
        N = 100000
        D = 64
        H = 128
        E = 25000
        key = jax.random.key(seed)
        k_nodes, k_edges, k_w1, k_w2 = jax.random.split(key, 4)
        nodes = jax.random.normal(k_nodes, (N, D), dtype=jnp.float32)
        edges = jax.random.randint(k_edges, (E, 2), 0, N, dtype=jnp.int32)
        W1 = jax.random.normal(k_w1, (2 * D, H), dtype=jnp.float32) * (1.0 / np.sqrt(2 * D))
        b1 = jnp.zeros((H,), dtype=jnp.float32)
        W2 = jax.random.normal(k_w2, (H, D), dtype=jnp.float32) * (1.0 / np.sqrt(H))
        b2 = jnp.zeros((D,), dtype=jnp.float32)
        return {'nodes': nodes, 'edges': edges, 'W1': W1, 'b1': b1, 'W2': W2, 'b2': b2}
    _L0_gnn_all = _L0_gnn_setup()
    _L0_gnn_in = {k: v for k, v in _L0_gnn_all.items() if k in ('W1', 'b1', 'W2', 'b2')}
    del _L0_gnn_all
    return {'x': x, 'src': src, 'dst': dst, 'L0_gnn_W1': _L0_gnn_in['W1'], 'L0_gnn_b1': _L0_gnn_in['b1'], 'L0_gnn_W2': _L0_gnn_in['W2'], 'L0_gnn_b2': _L0_gnn_in['b2']}

def reference(x, src, dst, L0_gnn_W1, L0_gnn_b1, L0_gnn_W2, L0_gnn_b2):
    import jax
    import jax.numpy as jnp

    def _L0_gnn_ref(nodes, edges, W1, b1, W2, b2):
        import jax, jax.numpy as jnp
        import numpy as np
        N = 100000
        D = 64
        H = 128
        E = 25000
        i = edges[:, 0]
        j = edges[:, 1]
        h_i = nodes[i]
        h_j = nodes[j]

        def mlp(x):
            return jax.nn.relu(x @ W1 + b1) @ W2 + b2
        m_ij = mlp(jnp.concatenate([h_i, h_j], axis=-1))
        m_ji = mlp(jnp.concatenate([h_j, h_i], axis=-1))
        out = nodes + jax.ops.segment_sum(m_ij, i, num_segments=N) + jax.ops.segment_sum(m_ji, j, num_segments=N)
        return out
    edge_index_t = jnp.stack([src, dst], axis=1)
    h = jnp.maximum(_layernorm(x, axis=-1), 0.0)
    x = x + _L0_gnn_ref(h, edge_index_t, L0_gnn_W1, L0_gnn_b1, L0_gnn_W2, L0_gnn_b2)
    return x

_drawn_inputs = setup_inputs


def setup_inputs(seed=0):
    import zlib

    import numpy as np

    out = dict(_drawn_inputs(seed))
    spreads = {'L0_gnn_b1': (0.0, 0.1), 'L0_gnn_b2': (0.0, 0.1)}
    factors = {}
    for name, (base, spread) in spreads.items():
        noise = np.random.default_rng([zlib.crc32(name.encode()), seed]).standard_normal(out[name].shape)
        drawn = base * np.exp(spread * noise) if base else spread * noise
        out[name] = jnp.asarray(drawn.astype(out[name].dtype))
    for name, factor in factors.items():
        out[name] = (out[name] * factor).astype(out[name].dtype)
    return out
```

```python
from contextlib import ExitStack

import concourse.bass as bass
from concourse import mybir

F32 = mybir.dt.float32
I32 = mybir.dt.int32
ALU = mybir.AluOpType
ACT = mybir.ActivationFunctionType
AX = mybir.AxisListType

P = 128
BANK = 512
ENDS = 2
TILES = 2
SLOTS = TILES * ENDS
EPS = 1e-5
FAR = 1 << 23


def gnn_layer(
    nc: bass.Bass,
    x: bass.AP,
    src: bass.AP,
    dst: bass.AP,
    W1: bass.AP,
    b1: bass.AP,
    W2: bass.AP,
    b2: bass.AP,
    out: bass.AP,
):
    N, D = x.shape
    E = src.shape[0]
    H = W1.shape[1]
    assert H == P and 2 * D == P
    COLS = -(-E // P)
    COLS += -COLS % (2 * TILES)
    LAST = E - (P - 1) * COLS
    assert 0 < LAST <= COLS
    BITS = COLS.bit_length()
    AHEAD = 2 * TILES
    R = 8
    CHUNK = P * R
    NCH = -(-N // CHUNK)
    NCH += NCH % 2
    START_LAST = N - CHUNK
    assert (NCH - 1) * CHUNK < N + CHUNK and (NCH - 1) * CHUNK <= N
    FILL = 64
    NF = N // (P * FILL)
    REST = N - NF * P * FILL
    REST_P = 32
    REST_R = REST // REST_P
    assert REST_P * REST_R == REST and REST_R <= FILL

    acc = [nc.dram_tensor(f"accumulator_{n}", [N + P, D], F32).ap() for n in ("src", "dst")]

    with ExitStack() as ctx:
        def sb(name, shape, dt=F32):
            return ctx.enter_context(nc.sbuf_tensor(name, shape, dt))

        def sem(name):
            return ctx.enter_context(nc.semaphore(name))

        ident = sb("ident", [P, P])
        ones = sb("ones", [P, P])
        before = sb("before", [P, P])
        spare = sb("spare", [P, 1])
        spare_i = sb("spare_i", [P, 1], I32)
        column = sb("column", [P, COLS])
        eps = sb("eps", [P, 1])
        w1 = sb("w1", [P, H])
        w1x = sb("w1x", [P, H])
        w1s = sb("w1s", [P, H])
        w2 = sb("w2", [P, D])
        b1c = sb("b1c", [P, 1])
        b2r = sb("b2r", [P, D])
        s_raw = sb("s_raw", [P, COLS], I32)
        d_raw = sb("d_raw", [P, COLS], I32)
        d_next = sb("d_next", [P, COLS], I32)
        loop_e = sb("loop_e", [P, COLS])
        falls = sb("falls", [P, COLS])
        keep = sb("keep", [P, COLS])
        drop = sb("drop", [P, COLS])
        shift = sb("shift", [P, COLS])
        shift_i = sb("shift_i", [P, COLS], I32)
        packed = sb("packed", [P, 2, COLS], I32)
        moves = sb("moves", [P, COLS], I32)
        edges = sb("edges", [P, COLS + AHEAD, ENDS], I32)
        counts = sb("counts", [P, 2])
        kept = sb("kept", [P, 1])
        flags = sb("flags", [P, 4])
        fills = sb("fills", [P, 2, FILL, D])
        rounds_f = sb("rounds_f", [1, 2])
        rounds_i = sb("rounds_i", [1, 2], I32)
        g_idx = [sb(f"g_idx{u}", [P, SLOTS], I32) for u in range(2)]
        f_idx = [sb(f"f_idx{u}", [P, SLOTS]) for u in range(2)]
        s_idx = [sb(f"s_idx{u}", [P, SLOTS], I32) for u in range(2)]
        rows = [sb(f"rows{u}", [P, SLOTS, D]) for u in range(2)]
        upd = [sb(f"upd{u}", [P, SLOTS, D]) for u in range(2)]
        same = sb("same", [P, SLOTS, P])
        same_b = sb("same_b", [P, SLOTS, P])
        dup = sb("dup", [P, SLOTS])
        away = sb("away", [P, SLOTS])
        e_sum = sb("e_sum", [P, SLOTS])
        e_cen = sb("e_cen", [P, SLOTS, D])
        e_sq = sb("e_sq", [P, SLOTS, D])
        e_var = sb("e_var", [P, SLOTS])
        e_std = sb("e_std", [P, SLOTS])
        e_inv = sb("e_inv", [P, SLOTS])
        e_h = sb("e_h", [P, SLOTS, D])
        e_hT = sb("e_hT", [P, TILES * P])
        e_hid = sb("e_hid", [P, ENDS, TILES, P])
        e_msg = sb("e_msg", [P, SLOTS, D])
        nx = [sb(f"nx{u}", [P, R, D]) for u in range(2)]
        na = [sb(f"na{u}", [P, R, D]) for u in range(2)]
        nd = [sb(f"nd{u}", [P, R, D]) for u in range(2)]
        n_sum = sb("n_sum", [P, R])
        n_cen = sb("n_cen", [P, R, D])
        n_sq = sb("n_sq", [P, R, D])
        n_var = sb("n_var", [P, R])
        n_std = sb("n_std", [P, R])
        n_inv = sb("n_inv", [P, R])
        n_h = [sb(f"n_h{u}", [P, R, D]) for u in range(2)]
        n_hT = [sb(f"n_hT{u}", [P, BANK]) for u in range(2)]
        n_hid = [sb(f"n_hid{u}", [P, 2, BANK]) for u in range(2)]
        n_add = [sb(f"n_add{u}", [P, R, D]) for u in range(2)]
        n_add2 = [sb(f"n_add2{u}", [P, R, D]) for u in range(2)]
        n_add3 = [sb(f"n_add3{u}", [P, R, D]) for u in range(2)]
        n_out = [sb(f"n_out{u}", [P, R, D]) for u in range(2)]
        bank = [ctx.enter_context(nc.psum_tensor(f"bank{b}", [P, BANK], F32)) for b in range(8)]

        padded = sem("padded")
        lists_in = sem("lists_in")
        weights_in = sem("weights_in")
        consts = sem("consts")
        sums = sem("sums")
        setup = sem("setup")
        filled = sem("filled")
        rounds_set = sem("rounds_set")
        g_idx_set = sem("g_idx_set")
        f_idx_set = sem("f_idx_set")
        gathered = [sem(f"gathered{u}") for u in range(2)]
        added = [sem(f"added_{n}") for n in ("src", "dst")]
        pool_steps = sem("pool_steps")
        scattered = sem("scattered")
        all_scattered = sem("all_scattered")
        idx_rows = sem("idx_rows")
        same_set = sem("same_set")
        before_set = sem("before_set")
        dup_set = sem("dup_set")
        away_set = sem("away_set")
        s_idx_set = sem("s_idx_set")
        e_summed = sem("e_summed")
        e_centred = sem("e_centred")
        e_squared = sem("e_squared")
        e_var_set = sem("e_var_set")
        e_std_set = sem("e_std_set")
        e_inv_set = sem("e_inv_set")
        e_h_set = sem("e_h_set")
        e_turned = sem("e_turned")
        e_hT_set = sem("e_hT_set")
        e_hid_made = sem("e_hid_made")
        e_hid_set = sem("e_hid_set")
        e_msg_made = sem("e_msg_made")
        e_msg_set = sem("e_msg_set")
        e_upd_made = sem("e_upd_made")
        e_upd_set = sem("e_upd_set")
        n_in = [sem(f"n_in{u}") for u in range(2)]
        n_stored = [sem(f"n_stored{u}") for u in range(2)]
        n_summed = sem("n_summed")
        n_centred = sem("n_centred")
        n_squared = sem("n_squared")
        n_var_set = sem("n_var_set")
        n_std_set = sem("n_std_set")
        n_inv_set = sem("n_inv_set")
        n_h_set = sem("n_h_set")
        n_turned = sem("n_turned")
        n_hT_set = sem("n_hT_set")
        n_hid_made = sem("n_hid_made")
        n_hid_set = sem("n_hid_set")
        n_msg_made = sem("n_msg_made")
        n_add_set = sem("n_add_set")
        n_add2_set = sem("n_add2_set")
        n_add3_set = sem("n_add3_set")
        n_out_set = sem("n_out_set")

        COUNTED = 7
        FILLS_MADE = COUNTED + 6
        KEPT = FILLS_MADE + 4
        SETUP_DONE = KEPT + 3 + 4 * BITS + 5 + 3 + 1
        N_FILLS = 2 * (NF + 1)
        ALL_WEIGHTS = 16 * 6
        ALL_CONSTS = 7
        MAX_ROUNDS = COLS // (2 * TILES)
        assert N << BITS < 1 << 31

        block = ctx.enter_context(nc.Block())

        def chunk_of(t, start):
            return t[bass.ds(start, CHUNK), :].rearrange("(p r) d -> p r d", p=P)

        def values(a):
            return a.rearrange("p s d -> p (s d)")

        @block.sync
        def _(sp):
            sp.wait_ge(padded, 3)
            for raw, first in ((s_raw, src), (d_raw, dst)):
                for lo, hi in ((0, 112), (112, P - 1)):
                    sp.dma_start(raw[lo:hi, :], first[lo * COLS:hi * COLS].rearrange("(p n) -> p n", n=COLS)
                                 ).then_inc(lists_in, 16)
                sp.dma_start(raw[P - 1:P, 0:LAST], first[(P - 1) * COLS:E][None, :]).then_inc(lists_in, 16)
            for lo, hi in ((0, 112), (112, P - 1)):
                sp.dma_start(d_next[lo:hi, :], dst[lo * COLS + 1:hi * COLS + 1].rearrange("(p n) -> p n", n=COLS)
                             ).then_inc(lists_in, 16)
            sp.dma_start(d_next[P - 1:P, 0:LAST - 1], dst[(P - 1) * COLS + 1:E][None, :]).then_inc(lists_in, 16)
            sp.wait_ge(setup, FILLS_MADE)
            for i in range(2):
                for c in range(NF):
                    sp.dma_start(acc[i][c * P * FILL:(c + 1) * P * FILL, :].rearrange("(p r) d -> p r d", p=P),
                                 fills[:, i]).then_inc(filled, 16)
                sp.dma_start(acc[i][NF * P * FILL:N, :].rearrange("(p r) d -> p r d", p=REST_P),
                             fills[0:REST_P, i, 0:REST_R]).then_inc(filled, 16)
            sp.wait_ge(all_scattered, 1)

            def load(u, start):
                sp.dma_start(nx[u][:], chunk_of(x, start)).then_inc(n_in[u], 16)
                sp.dma_start(na[u][:], chunk_of(acc[0], start)).then_inc(n_in[u], 16)
                sp.dma_start(nd[u][:], chunk_of(acc[1], start)).then_inc(n_in[u], 16)

            for u in range(2):
                load(u, u * CHUNK)
            with sp.Fori(1, NCH // 2 - 1) as k:
                for u in range(2):
                    sp.wait_ge(n_centred, k * 2 + (u - 1))
                    sp.wait_ge(n_add2_set, k * 2 + (u - 1))
                    load(u, k * (2 * CHUNK) + u * CHUNK)
            for u in range(2):
                sp.wait_ge(n_centred, NCH - 3 + u)
                sp.wait_ge(n_add2_set, NCH - 3 + u)
                load(u, (NCH - 2) * CHUNK if u == 0 else START_LAST)

        @block.gpsimd
        def _(pool):
            nc.gpsimd.iota(column[:], [[1, COLS]], base=0, channel_multiplier=0,
                           allow_small_or_imprecise_dtypes=True).then_inc(consts, 1)
            nc.gpsimd.iota(spare[:], [[0, 1]], base=N, channel_multiplier=1,
                           allow_small_or_imprecise_dtypes=True).then_inc(consts, 1)
            nc.gpsimd.iota(spare_i[:], [[0, 1]], base=N, channel_multiplier=1).then_inc(consts, 1)
            nc.gpsimd.memset(ones[:], 1.0).then_inc(consts, 1)
            nc.gpsimd.memset(eps[:], EPS).then_inc(consts, 1)
            pool.wait_ge(consts, 4)
            nc.gpsimd.affine_select(out=ident[:], in_=ones[:], compare_op=ALU.is_equal, fill=0.0, base=0,
                                    pattern=[[-1, P]], channel_multiplier=1).then_inc(consts, 1)
            nc.gpsimd.affine_select(out=before[:], in_=ones[:], compare_op=ALU.is_gt, fill=0.0, base=0,
                                    pattern=[[-1, P]], channel_multiplier=1).then_inc(consts, 1)
            pool.wait_ge(setup, FILLS_MADE)
            for i in range(2):
                pool.dma_start(acc[i][N:N + P, :], fills[:, i, 0, :]).then_inc(added[i], 16)
            pool.sem_inc(scattered, 1)

            def gather(u, s):
                pool.indirect_dma_start(
                    out=rows[u][:, s, :], out_offset=None, in_=x[:, :],
                    in_offset=bass.IndirectOffsetOnAxis(ap=g_idx[u][:, s:s + 1], axis=0)).then_inc(gathered[u], 16)

            def scatter(u, s, done):
                pool.wait_ge(added[s % ENDS], done)
                pool.sem_inc(pool_steps, 1)
                pool.indirect_dma_start(
                    out=acc[s % ENDS][:, :],
                    out_offset=bass.IndirectOffsetOnAxis(ap=s_idx[u][:, s:s + 1], axis=0),
                    in_=upd[u][:, s, :], in_offset=None, compute_op=ALU.add).then_inc(added[s % ENDS], 16)

            def scatter_tile(u, t, k):
                if t == 0:
                    pool.wait_ge(e_upd_set, k * 2 + (u + 1))
                    pool.wait_ge(s_idx_set, k * 2 + (u + 1))
                    pool.sem_inc(pool_steps, 1)
                for end in range(ENDS):
                    scatter(u, ENDS * t + end, k * (16 * 2 * TILES) + 16 * (u * TILES + t + 1))
                if t == 0:
                    pool.sem_inc(scattered, 1)

            pool.wait_ge(rounds_set, 1)
            more = pool.value_load(rounds_i[0:1, 0:1], min_val=0, max_val=MAX_ROUNDS - 2)
            for u in range(2):
                pool.wait_ge(g_idx_set, u + 1)
                for s in range(SLOTS):
                    gather(u, s)
            pool.wait_ge(filled, 16 * N_FILLS)
            with pool.Fori(0, more + 1) as k:
                for u in range(2):
                    pool.wait_ge(g_idx_set, k * 2 + (u + 3))
                    pool.wait_ge(e_centred, k * 2 + (u + 1))
                    pool.sem_inc(pool_steps, 1)
                    for t in range(TILES):
                        for end in range(ENDS):
                            gather(u, ENDS * t + end)
                        scatter_tile(u, t, k)
            for u in range(2):
                for t in range(TILES):
                    scatter_tile(u, t, more + 1)
            for i in range(ENDS):
                pool.wait_ge(added[i], more * (16 * 2 * TILES) + 16 * (2 * 2 * TILES + 1))
            pool.sem_inc(all_scattered, 1)

            def sums_of(u, chunk, turn):
                pool.wait_ge(n_in[u], turn * 48 + 48)
                nc.gpsimd.tensor_tensor(n_add[u][:], na[u][:], nd[u][:], ALU.add).then_inc(n_add_set, 1)
                pool.wait_ge(n_add_set, chunk + 1)
                nc.gpsimd.tensor_tensor(n_add2[u][:], n_add[u][:], nx[u][:], ALU.add).then_inc(n_add2_set, 1)
                pool.wait_ge(n_add2_set, chunk + 1)
                pool.wait_ge(n_h_set, chunk + 1)
                nc.gpsimd.tensor_tensor(n_add3[u][:], n_add2[u][:], n_h[u][:], ALU.add).then_inc(n_add3_set, 1)

            for u in range(2):
                sums_of(u, u, 0)
            with pool.Fori(1, NCH // 2) as k:
                for u in range(2):
                    pool.wait_ge(n_out_set, k * 2 + (u - 1))
                    sums_of(u, k * 2 + u, k)

        @block.scalar
        def _(act):
            act.dma_start(w1[:], W1).then_inc(weights_in, 16)
            act.dma_start(w1x[0:D, :], W1[D:2 * D, :]).then_inc(weights_in, 16)
            act.dma_start(w1x[D:2 * D, :], W1[0:D, :]).then_inc(weights_in, 16)
            act.dma_start(w2[:], W2).then_inc(weights_in, 16)
            act.dma_start(b1c[:], b1[:, None]).then_inc(weights_in, 16)
            act.dma_start(b2r[:], b2.partition_broadcast(P)).then_inc(weights_in, 16)
            act.wait_ge(weights_in, ALL_WEIGHTS)
            act.wait_ge(consts, ALL_CONSTS)
            act.wait_ge(rounds_set, 1)
            more = act.value_load(rounds_i[0:1, 0:1], min_val=0, max_val=MAX_ROUNDS - 2)
            with act.Fori(0, more + 2) as k:
                for u in range(2):
                    n = k * 2 + (u + 1)
                    act.wait_ge(e_centred, n)
                    nc.scalar.activation(e_sq[:], e_cen[:], ACT.Square).then_inc(e_squared, 1)
                    act.wait_ge(e_var_set, n)
                    nc.scalar.activation(e_std[:], e_var[:], ACT.Sqrt, bias=eps[:], scale=1.0 / D
                                         ).then_inc(e_std_set, 1)
                    act.wait_ge(e_turned, n)
                    nc.scalar.copy(e_hT[:], bank[1][:, 0:TILES * P]).then_inc(e_hT_set, 1)
                    act.wait_ge(e_hid_made, n)
                    nc.scalar.activation(e_hid[:].rearrange("p e t n -> p (e t n)"), bank[2][:], ACT.Relu,
                                         bias=b1c[:]).then_inc(e_hid_set, 1)
                    act.wait_ge(scattered, n)
                    act.wait_ge(e_upd_made, n)
                    nc.scalar.copy(values(upd[u][:]), bank[4][:, 0:SLOTS * D]).then_inc(e_upd_set, 1)

            def square(chunk):
                act.wait_ge(n_centred, chunk + 1)
                nc.scalar.activation(n_sq[:], n_cen[:], ACT.Square).then_inc(n_squared, 1)

            def root(chunk):
                act.wait_ge(n_var_set, chunk + 1)
                nc.scalar.activation(n_std[:], n_var[:], ACT.Sqrt, bias=eps[:], scale=1.0 / D
                                     ).then_inc(n_std_set, 1)

            def turned(u, chunk):
                act.wait_ge(n_turned, chunk + 1)
                nc.scalar.copy(n_hT[u][:], bank[u][:]).then_inc(n_hT_set, 1)

            def hidden(u, chunk):
                for half in range(2):
                    act.wait_ge(n_hid_made, chunk * 2 + (half + 1))
                    nc.scalar.activation(n_hid[u][:, half], bank[2 + 2 * u + half][:], ACT.Relu, bias=b1c[:]
                                         ).then_inc(n_hid_set, 1)

            def store(u, chunk, start):
                act.wait_ge(n_out_set, chunk + 1)
                act.dma_start(chunk_of(out, start), n_out[u][:]).then_inc(n_stored[u], 16)

            def act_step(u, chunk, first=False, last=False):
                if not last:
                    square(chunk + 1)
                if not first:
                    store(1 - u, chunk - 1, (chunk - 1) * CHUNK)
                turned(u, chunk)
                if not last:
                    root(chunk + 1)
                hidden(u, chunk)

            square(0)
            root(0)
            for u in range(2):
                act_step(u, u, first=(u == 0))
            with act.Fori(1, NCH // 2 - 1) as k:
                for u in range(2):
                    act_step(u, k * 2 + u)
            act_step(0, NCH - 2)
            act_step(1, NCH - 1, last=True)
            act.wait_ge(n_stored[0], 16 * (NCH // 2))
            store(1, NCH - 1, START_LAST)
            act.wait_ge(n_stored[1], 16 * (NCH // 2))

        @block.vector
        def _(dve):
            count = [0]

            def step(ins):
                count[0] += 1
                ins.then_inc(setup, 1)
                dve.wait_ge(setup, count[0])

            nc.vector.memset(s_raw[:], -1).then_inc(padded, 1)
            nc.vector.memset(d_raw[:], -1).then_inc(padded, 1)
            nc.vector.memset(d_next[:], FAR).then_inc(padded, 1)
            dve.wait_ge(lists_in, 16 * 9)
            step(nc.vector.tensor_tensor(loop_e[:], s_raw[:], d_raw[:], ALU.is_equal))
            step(nc.vector.tensor_tensor(drop[:], d_raw[:], d_next[:], ALU.not_equal))
            step(nc.vector.tensor_tensor(loop_e[:], loop_e[:], drop[:], ALU.mult))
            step(nc.vector.scalar_tensor_tensor(out=loop_e[:], in0=s_raw[:], scalar=0.0, in1=loop_e[:],
                                                op0=ALU.is_ge, op1=ALU.mult))
            step(nc.vector.tensor_tensor(falls[:], d_raw[:], d_next[:], ALU.is_gt))
            step(nc.vector.tensor_reduce(counts[:, 0:1], loop_e[:], AX.X, ALU.add))
            step(nc.vector.tensor_reduce(counts[:, 1:2], falls[:], AX.X, ALU.add))
            assert count[0] == COUNTED
            dve.wait_ge(sums, 1)
            step(nc.vector.tensor_scalar(flags[:, 0:1], bank[7][:, 0:1], float(N), None, ALU.is_equal))
            step(nc.vector.tensor_scalar(flags[:, 1:2], bank[7][:, 1:2], 0.0, None, ALU.is_equal))
            step(nc.vector.scalar_tensor_tensor(out=flags[:, 2:3], in0=flags[:, 0:1], scalar=2.0,
                                                in1=flags[:, 1:2], op0=ALU.mult, op1=ALU.mult))
            step(nc.vector.tensor_scalar(flags[:, 3:4], flags[:, 2:3], -0.5, None, ALU.mult))
            dve.wait_ge(weights_in, ALL_WEIGHTS)
            step(nc.vector.tensor_scalar(fills[:, 0], b2r[:].unsqueeze(1).to_broadcast([P, FILL, D]),
                                         flags[:, 2:3], None, ALU.mult))
            step(nc.vector.memset(fills[:, 1], 0.0))
            assert count[0] == FILLS_MADE
            step(nc.vector.tensor_scalar(drop[:], s_raw[:], 0.0, None, ALU.is_ge))
            step(nc.vector.scalar_tensor_tensor(out=keep[:], in0=loop_e[:], scalar=flags[:, 3:4], in1=drop[:],
                                                op0=ALU.mult, op1=ALU.add))
            step(nc.vector.tensor_scalar(drop[:], keep[:], -1.0, 1.0, ALU.mult, ALU.add))
            step(nc.vector.tensor_reduce(kept[:], keep[:], AX.X, ALU.add))
            assert count[0] == KEPT
            step(nc.vector.tensor_tensor_scan(shift[:], drop[:], drop[:], 0.0, ALU.add, ALU.max))
            step(nc.vector.tensor_tensor(shift_i[:], shift[:], keep[:], ALU.mult))
            step(nc.vector.scalar_tensor_tensor(out=packed[:, 0], in0=s_raw[:], scalar=BITS, in1=shift_i[:],
                                                op0=ALU.logical_shift_left, op1=ALU.bitwise_or))
            for b in range(BITS):
                old, new, far = packed[:, b % 2], packed[:, (b + 1) % 2], 1 << b
                step(nc.vector.tensor_scalar(moves[:], old, 31 - b, 31, ALU.logical_shift_left,
                                             ALU.arith_shift_right))
                step(nc.vector.scalar_tensor_tensor(out=new, in0=moves[:], scalar=-1, in1=old,
                                                    op0=ALU.bitwise_xor, op1=ALU.bitwise_and))
                step(nc.vector.copy_predicated(new[:, 0:COLS - far], moves[:, far:], old[:, far:]))
                step(nc.vector.copy_predicated(d_raw[:, 0:COLS - far], moves[:, far:], d_raw[:, far:]))
            step(nc.vector.tensor_scalar(edges[:, 0:COLS, 0], packed[:, BITS % 2], BITS, None,
                                         ALU.arith_shift_right))
            step(nc.vector.tensor_copy(edges[:, 0:COLS, 1], d_raw[:]))
            step(nc.vector.tensor_copy(values(edges[:, COLS:, :]), spare_i[:].to_broadcast([P, AHEAD * ENDS])))
            step(nc.vector.tensor_scalar(moves[:], column[:], kept[:, 0:1], None, ALU.is_ge))
            step(nc.vector.copy_predicated(edges[:, 0:COLS, :], moves[:].unsqueeze(2).to_broadcast([P, COLS, ENDS]),
                                           spare_i[:].unsqueeze(2).to_broadcast([P, COLS, ENDS])))
            dve.wait_ge(sums, 2)
            step(nc.vector.tensor_reduce(rounds_f[:, 0:1], bank[6][0:1, 0:P], AX.X, ALU.max))
            step(nc.vector.tensor_scalar(rounds_f[:, 1:2], rounds_f[:, 0:1], float(2 * TILES - 1 - 2 * 2 * TILES), 0.0,
                                         ALU.add, ALU.max))
            step(nc.vector.tensor_copy(rounds_i[:, 1:2], rounds_f[:, 1:2]))
            nc.vector.tensor_scalar(rounds_i[:, 0:1], rounds_i[:, 1:2], (2 * TILES).bit_length() - 1, None,
                                    ALU.arith_shift_right).then_inc(rounds_set, 1)
            step(nc.vector.tensor_tensor(w1s[:], w1[:], w1x[:], ALU.add))

            def prepare(u, first):
                cols = edges[:, bass.ds(first, TILES), :].rearrange("p t e -> p (t e)")
                nc.vector.tensor_scalar(g_idx[u][:], cols, float(N - 1), None, ALU.min).then_inc(g_idx_set, 1)
                nc.vector.tensor_copy(f_idx[u][:], cols).then_inc(f_idx_set, 1)

            dve.wait_ge(rounds_set, 1)
            more = dve.value_load(rounds_i[0:1, 0:1], min_val=0, max_val=MAX_ROUNDS - 2)
            for u in range(2):
                prepare(u, TILES * u)

            def each(a):
                return a.unsqueeze(2).to_broadcast([a.shape[0], a.shape[1], D])

            with dve.Fori(0, more + 2) as k:
                for u in range(2):
                    n = k * 2 + (u + 1)
                    dve.wait_ge(gathered[u], (k + 1) * (16 * SLOTS))
                    nc.vector.tensor_reduce(e_sum[:], rows[u][:], AX.X, ALU.add).then_inc(e_summed, 1)
                    dve.wait_ge(e_summed, n)
                    nc.vector.scalar_tensor_tensor(out=e_cen[:], in0=each(e_sum[:]), scalar=-1.0 / D,
                                                   in1=rows[u][:], op0=ALU.mult, op1=ALU.add
                                                   ).then_inc(e_centred, 1)
                    dve.wait_ge(f_idx_set, n)
                    dve.wait_ge(idx_rows, n)
                    nc.vector.tensor_tensor(same[:], bank[0][:].rearrange("p (s q) -> p s q", s=SLOTS),
                                            f_idx[u][:].unsqueeze(2).to_broadcast([P, SLOTS, P]),
                                            ALU.is_equal).then_inc(same_set, 1)
                    dve.wait_ge(e_squared, n)
                    nc.vector.tensor_reduce(e_var[:], e_sq[:], AX.X, ALU.add).then_inc(e_var_set, 1)
                    dve.wait_ge(same_set, n)
                    nc.vector.tensor_tensor(same_b[:], same[:], before[:].unsqueeze(1).to_broadcast([P, SLOTS, P]),
                                            ALU.mult).then_inc(before_set, 1)
                    dve.wait_ge(e_std_set, n)
                    nc.vector.reciprocal(e_inv[:], e_std[:]).then_inc(e_inv_set, 1)
                    dve.wait_ge(e_inv_set, n)
                    dve.wait_ge(e_centred, n)
                    nc.vector.scalar_tensor_tensor(out=e_h[:], in0=e_cen[:], scalar=0.0, in1=each(e_inv[:]),
                                                   op0=ALU.max, op1=ALU.mult).then_inc(e_h_set, 1)
                    dve.wait_ge(before_set, n)
                    nc.vector.tensor_reduce(dup[:], same_b[:], AX.X, ALU.add).then_inc(dup_set, 1)
                    dve.wait_ge(dup_set, n)
                    nc.vector.scalar_tensor_tensor(out=away[:], in0=dup[:], scalar=0.0,
                                                   in1=spare[:].to_broadcast([P, SLOTS]),
                                                   op0=ALU.is_gt, op1=ALU.mult).then_inc(away_set, 1)
                    dve.wait_ge(away_set, n)
                    dve.wait_ge(scattered, n)
                    nc.vector.tensor_tensor(s_idx[u][:], f_idx[u][:], away[:], ALU.max).then_inc(s_idx_set, 1)
                    dve.wait_ge(s_idx_set, n)
                    prepare(u, k * (2 * TILES) + (2 + u) * TILES)
                    dve.wait_ge(e_msg_made, n)
                    nc.vector.tensor_tensor(e_msg[:], bank[3][:, 0:SLOTS * D].rearrange("p (s d) -> p s d", s=SLOTS),
                                            b2r[:].unsqueeze(1).to_broadcast([P, SLOTS, D]), ALU.add
                                            ).then_inc(e_msg_set, 1)

            def centre(u, chunk, turn):
                dve.wait_ge(n_in[u], turn * 48 + 48)
                nc.vector.tensor_reduce(n_sum[:], nx[u][:], AX.X, ALU.add).then_inc(n_summed, 1)
                dve.wait_ge(n_summed, chunk + 1)
                nc.vector.scalar_tensor_tensor(out=n_cen[:], in0=each(n_sum[:]), scalar=-1.0 / D, in1=nx[u][:],
                                               op0=ALU.mult, op1=ALU.add).then_inc(n_centred, 1)

            def normalise(u, chunk):
                dve.wait_ge(n_squared, chunk + 1)
                nc.vector.tensor_reduce(n_var[:], n_sq[:], AX.X, ALU.add).then_inc(n_var_set, 1)
                dve.wait_ge(n_std_set, chunk + 1)
                nc.vector.reciprocal(n_inv[:], n_std[:]).then_inc(n_inv_set, 1)
                dve.wait_ge(n_inv_set, chunk + 1)
                nc.vector.scalar_tensor_tensor(out=n_h[u][:], in0=n_cen[:], scalar=0.0, in1=each(n_inv[:]),
                                               op0=ALU.max, op1=ALU.mult).then_inc(n_h_set, 1)

            def finish(u, chunk):
                dve.wait_ge(n_msg_made, chunk + 1)
                dve.wait_ge(n_add3_set, chunk + 1)
                nc.vector.scalar_tensor_tensor(out=n_out[u][:],
                                               in0=bank[6 + u][:].rearrange("p (r d) -> p r d", r=R),
                                               scalar=flags[:, 2:3], in1=n_add3[u][:], op0=ALU.mult,
                                               op1=ALU.add).then_inc(n_out_set, 1)

            def dve_step(u, chunk, turn, first=False, last=False):
                if not last:
                    centre(1 - u, chunk + 1, turn + u)
                    normalise(1 - u, chunk + 1)
                if not first:
                    dve.wait_ge(n_stored[u], turn * 16)
                finish(u, chunk)

            centre(0, 0, 0)
            normalise(0, 0)
            for u in range(2):
                dve_step(u, u, 0, first=True)
            with dve.Fori(1, NCH // 2 - 1) as k:
                for u in range(2):
                    dve_step(u, k * 2 + u, k)
            dve_step(0, NCH - 2, NCH // 2 - 1)
            dve_step(1, NCH - 1, NCH // 2 - 1, last=True)
            assert count[0] == SETUP_DONE

        @block.tensor
        def _(pe):
            pe.wait_ge(consts, ALL_CONSTS)
            pe.wait_ge(setup, COUNTED)
            nc.tensor.matmul(bank[7][:, 0:2], ones[:], counts[:], start=True, stop=True).then_inc(sums, 1)
            pe.wait_ge(setup, KEPT)
            nc.tensor.transpose(bank[6][0:1, 0:P], kept[:], ident[:]).then_inc(sums, 1)
            pe.wait_ge(weights_in, ALL_WEIGHTS)
            pe.wait_ge(rounds_set, 1)
            more = pe.value_load(rounds_i[0:1, 0:1], min_val=0, max_val=MAX_ROUNDS - 2)
            with pe.Fori(0, more + 2) as k:
                for u in range(2):
                    n = k * 2 + (u + 1)
                    pe.wait_ge(f_idx_set, n)
                    for s in range(SLOTS):
                        last = nc.tensor.transpose(bank[0][:, s * P:(s + 1) * P],
                                                   f_idx[u][:, s:s + 1].to_broadcast([P, P]), ident[:])
                    last.then_inc(idx_rows, 1)
                    pe.wait_ge(e_h_set, n)
                    for t in range(TILES):
                        last = nc.tensor.transpose(bank[1][:, t * P:(t + 1) * P],
                                                   values(e_h[:, ENDS * t:ENDS * (t + 1), :]), ident[:])
                    last.then_inc(e_turned, 1)
                    pe.wait_ge(e_hT_set, n)
                    for end, w in enumerate((w1, w1x)):
                        last = nc.tensor.matmul(bank[2][:, end * TILES * P:(end + 1) * TILES * P], w[:], e_hT[:],
                                                start=True, stop=True)
                    last.then_inc(e_hid_made, 1)
                    pe.wait_ge(e_hid_set, n)
                    for t in range(TILES):
                        for end in range(ENDS):
                            s = ENDS * t + end
                            last = nc.tensor.matmul(bank[3][:, s * D:(s + 1) * D], e_hid[:, end, t, :], w2[:],
                                                    start=True, stop=True)
                    last.then_inc(e_msg_made, 1)
                    pe.wait_ge(e_msg_set, n)
                    pe.wait_ge(same_set, n)
                    for s in range(SLOTS):
                        last = nc.tensor.matmul(bank[4][:, s * D:(s + 1) * D], same[:, s, :], e_msg[:, s, :],
                                                start=True, stop=True)
                    last.then_inc(e_upd_made, 1)

            def turn(u, chunk):
                pe.wait_ge(n_h_set, chunk + 1)
                for r in range(R // 2):
                    last = nc.tensor.transpose(bank[u][:, r * P:(r + 1) * P],
                                               values(n_h[u][:, 2 * r:2 * r + 2, :]), ident[:])
                last.then_inc(n_turned, 1)

            def hidden(u, chunk):
                pe.wait_ge(n_hT_set, chunk + 1)
                for half in range(2):
                    part = slice(half * D, half * D + D)
                    nc.tensor.matmul(bank[2 + 2 * u + half][:], w1s[part, :], n_hT[u][part, :],
                                     start=True, stop=True).then_inc(n_hid_made, 1)

            def message(u, chunk):
                for half in range(2):
                    pe.wait_ge(n_hid_set, chunk * 2 + (half + 1))
                    for r in range(R // 2):
                        o = (2 * r + half) * D
                        last = nc.tensor.matmul(bank[6 + u][:, o:o + D], n_hid[u][:, half, r * P:(r + 1) * P],
                                                w2[:], start=True, stop=True)
                last.then_inc(n_msg_made, 1)

            def pe_step(u, chunk, first=False, last=False):
                hidden(u, chunk)
                if not last:
                    turn(1 - u, chunk + 1)
                if not first:
                    pe.wait_ge(n_out_set, chunk - 1)
                message(u, chunk)

            pe.wait_ge(setup, SETUP_DONE)
            turn(0, 0)
            for u in range(2):
                pe_step(u, u, first=True)
            with pe.Fori(1, NCH // 2 - 1) as k:
                for u in range(2):
                    pe_step(u, k * 2 + u)
            pe_step(0, NCH - 2)
            pe_step(1, NCH - 1, last=True)


_INS = ["x", "src", "dst", "L0_gnn_W1", "L0_gnn_b1", "L0_gnn_W2", "L0_gnn_b2"]


def kernel(**inputs):
    import numpy as _np
    import concourse.bacc as _bacc
    from concourse import mybir as _mybir
    from concourse.bass_utils import run_bass_kernel_spmd as _run

    nc = _bacc.Bacc("TRN2", target_bir_lowering=False, num_devices=1)
    arrays, args = {}, []
    for name in _INS:
        a = _np.ascontiguousarray(inputs[name])
        arrays[f"in_{name}_dram"] = a
        args.append(nc.dram_tensor(f"in_{name}_dram", a.shape, _mybir.dt.from_np(a.dtype), kind="ExternalInput").ap())
    out = nc.dram_tensor("out_dram", arrays["in_x_dram"].shape, _mybir.dt.float32, kind="ExternalOutput").ap()
    gnn_layer(nc, *args, out)
    r = _run(nc, [arrays], core_ids=[0])
    return r.results[0]["out_dram"]
```

```python
from contextlib import ExitStack

import concourse.bass as bass
from concourse import mybir

F32 = mybir.dt.float32
BF16 = mybir.dt.bfloat16
I32 = mybir.dt.int32
ALU = mybir.AluOpType
ACT = mybir.ActivationFunctionType
AX = mybir.AxisListType

P = 128
BANK = 512
ENDS = 2
TILES = 2
SLOTS = TILES * ENDS
PER_ROUND = 2
PARTS = 3
EPS = 1e-5
FAR = 1 << 23


def gnn_layer(
    nc: bass.Bass,
    x: bass.AP,
    src: bass.AP,
    dst: bass.AP,
    W1: bass.AP,
    b1: bass.AP,
    W2: bass.AP,
    b2: bass.AP,
    out: bass.AP,
):
    N, D = x.shape
    E = src.shape[0]
    H = W1.shape[1]
    assert H == P and 2 * D == P
    ROUND = PER_ROUND * TILES
    COLS = -(-E // P)
    COLS += -COLS % ROUND
    LAST = E - (P - 1) * COLS
    assert 1 < LAST <= COLS
    BITS = COLS.bit_length()
    assert N << BITS < 1 << 31
    BLOCKS = -(-(COLS + 4 * TILES) * ENDS // P)
    WIDE = BLOCKS * P // ENDS
    R = 8
    CHUNK = P * R
    NCH = -(-N // CHUNK)
    NCH += NCH % 2
    OVER = NCH * CHUNK - N
    assert 0 <= OVER <= CHUNK
    LEAST = NCH + 2
    MOST = COLS // ROUND
    assert LEAST < MOST
    FILL = 25
    NF = N // (P * FILL)
    REST = N - NF * P * FILL
    REST_P = 32
    REST_R = REST // REST_P
    assert REST_P * REST_R == REST and REST_R <= FILL
    FC = 2
    FB = 3
    STEPS = (NCH - FC) // FC
    assert STEPS % FB == 0 and NCH % FC == 0

    acc = [nc.dram_tensor(f"accumulator_{n}", [N + P, D], F32).ap() for n in ("src", "dst")]
    dense = nc.dram_tensor("dense", [NCH * CHUNK, D], F32).ap()
    tile_rows = nc.dram_tensor("tile_rows", [WIDE * ENDS, P], F32).ap()

    with ExitStack() as ctx:
        def sb(name, shape, dt=F32):
            return ctx.enter_context(nc.sbuf_tensor(name, shape, dt))

        def sem(name):
            return ctx.enter_context(nc.semaphore(name))

        ident = sb("ident", [P, P])
        ones = sb("ones", [P, P])
        before = sb("before", [P, P], BF16)
        spare = sb("spare", [P, 1])
        column = sb("column", [P, COLS])
        eps = sb("eps", [P, 1])
        root_of = sb("root_of", [P, 1])
        w1 = sb("w1", [P, H])
        w1x = sb("w1x", [P, H])
        w1s = sb("w1s", [P, H])
        w2 = sb("w2", [P, D])
        b1c = sb("b1c", [P, 1])
        b2r = sb("b2r", [P, D])
        s_raw = sb("s_raw", [P, COLS], I32)
        d_raw = sb("d_raw", [P, COLS], I32)
        d_next = sb("d_next", [P, COLS], I32)
        loop_e = sb("loop_e", [P, COLS])
        drop = sb("drop", [P, COLS])
        keep = sb("keep", [P, COLS])
        shift_i = sb("shift_i", [P, COLS], I32)
        packed = sb("packed", [P, 2, COLS], I32)
        moves = sb("moves", [P, COLS], I32)
        edges = sb("edges", [P, WIDE, ENDS])
        turned_list = sb("turned_list", [P, BLOCKS, P])
        counts = sb("counts", [P, 2])
        kept = sb("kept", [P, 1])
        flags = sb("flags", [P, 4])
        zero_fill = sb("zero_fill", [P, FILL, D])
        b2_fill = sb("b2_fill", [P, FILL, D])
        rounds_f = sb("rounds_f", [1, 2])
        rounds_i = sb("rounds_i", [1, 2], I32)
        g_idx = [sb(f"g_idx{u}", [P, SLOTS], I32) for u in range(2)]
        s_idx = [sb(f"s_idx{u}", [P, SLOTS], I32) for u in range(2)]
        rows = [sb(f"rows{u}", [P, SLOTS, D]) for u in range(2)]
        upd = [sb(f"upd{u}", [P, SLOTS, D]) for u in range(2)]
        ends = [sb(f"ends{u}", [P, SLOTS, P]) for u in range(2)]
        same = [sb(f"same{u}", [P, SLOTS, P], BF16) for u in range(2)]
        same_b = sb("same_b", [P, SLOTS, P], BF16)
        dup = sb("dup", [P, SLOTS])
        away = sb("away", [P, SLOTS])
        e_sum = sb("e_sum", [P, SLOTS])
        e_cen = sb("e_cen", [P, SLOTS, D])
        e_sq = sb("e_sq", [P, SLOTS, D])
        e_var = sb("e_var", [P, SLOTS])
        e_std = sb("e_std", [P, SLOTS])
        e_inv = sb("e_inv", [P, SLOTS])
        e_h = sb("e_h", [P, SLOTS, D])
        e_hT = sb("e_hT", [P, TILES * P])
        e_hid = sb("e_hid", [P, ENDS, TILES, P])
        e_msg = sb("e_msg", [P, SLOTS, D])
        e_rest = sb("e_rest", [P, SLOTS, D])
        e_part = sb("e_part", [P, PARTS, SLOTS, D], BF16)
        nx = sb("nx", [P, R, D])
        n_sum = sb("n_sum", [P, R])
        n_cen = sb("n_cen", [P, R, D])
        n_sq = sb("n_sq", [P, R, D])
        n_var = sb("n_var", [P, R])
        n_std = sb("n_std", [P, R])
        n_inv = sb("n_inv", [P, R])
        n_h = sb("n_h", [P, R, D])
        n_xh = sb("n_xh", [P, R, D])
        n_hT = sb("n_hT", [P, BANK])
        n_hid = sb("n_hid", [P, 2, BANK])
        n_out = sb("n_out", [P, R, D])
        fs = [sb(f"fs{b}", [P, FC, R, D]) for b in range(FB)]
        fd = [sb(f"fd{b}", [P, FC, R, D]) for b in range(FB)]
        fn = [sb(f"fn{b}", [P, FC, R, D]) for b in range(FB)]
        bank = [ctx.enter_context(nc.psum_tensor(f"bank{b}", [P, BANK], F32)) for b in range(8)]
        E_TURN, E_HID, E_MSG, E_UPD, N_TURN, N_HID, N_MSG = bank[0], bank[1], bank[2], bank[3], bank[4], bank[5:7], bank[7]

        padded = sem("padded")
        lists_in = sem("lists_in")
        weights_in = sem("weights_in")
        consts = sem("consts")
        zeroed = sem("zeroed")
        sums = sem("sums")
        setup = sem("setup")
        list_turned = sem("list_turned")
        list_copied = sem("list_copied")
        list_stored = sem("list_stored")
        filled = sem("filled")
        rounds_set = sem("rounds_set")
        root_table = sem("root_table")
        g_idx_set = sem("g_idx_set")
        gathered = [sem(f"gathered{u}") for u in range(2)]
        added = [sem(f"added_{n}") for n in ("src", "dst")]
        pool_steps = sem("pool_steps")
        scattered = sem("scattered")
        all_scattered = sem("all_scattered")
        ends_in = [sem(f"ends_in{u}") for u in range(2)]
        same_set = sem("same_set")
        before_set = sem("before_set")
        dup_set = sem("dup_set")
        away_set = sem("away_set")
        s_idx_set = sem("s_idx_set")
        e_summed = sem("e_summed")
        e_centred = sem("e_centred")
        e_squared = sem("e_squared")
        e_var_set = sem("e_var_set")
        e_std_set = sem("e_std_set")
        e_inv_set = sem("e_inv_set")
        e_h_set = sem("e_h_set")
        e_turned = sem("e_turned")
        e_hT_set = sem("e_hT_set")
        e_hid_made = sem("e_hid_made")
        e_hid_set = sem("e_hid_set")
        e_msg_made = sem("e_msg_made")
        e_msg_set = sem("e_msg_set")
        e_part_set = sem("e_part_set")
        e_rest_set = sem("e_rest_set")
        e_split_set = sem("e_split_set")
        e_upd_made = sem("e_upd_made")
        e_upd_set = sem("e_upd_set")
        n_in = sem("n_in")
        n_summed = sem("n_summed")
        n_centred = sem("n_centred")
        n_squared = sem("n_squared")
        n_var_set = sem("n_var_set")
        n_std_set = sem("n_std_set")
        n_inv_set = sem("n_inv_set")
        n_h_set = sem("n_h_set")
        n_xh_set = sem("n_xh_set")
        n_turned = sem("n_turned")
        n_hT_set = sem("n_hT_set")
        n_hid_made = sem("n_hid_made")
        n_hid_set = sem("n_hid_set")
        n_msg_made = sem("n_msg_made")
        n_out_set = sem("n_out_set")
        n_stored = sem("n_stored")
        n_out_free = sem("n_out_free")
        f_in = [sem(f"f_in{b}") for b in range(FB)]
        f_stored = [sem(f"f_stored{b}") for b in range(FB)]
        f_summed = sem("f_summed")
        f_out_set = sem("f_out_set")

        COUNTED = 7
        FILL_MADE = COUNTED + 5
        KEPT = FILL_MADE + 4
        LISTED = KEPT + 3 + 4 * BITS + 7
        SETUP_DONE = LISTED + 3 + 1
        N_FILLS = 2 * (NF + 1)
        ALL_WEIGHTS = 16 * 6
        ALL_CONSTS = 6
        GROUPS = [list(range(b, min(b + 4, BLOCKS))) for b in range(0, BLOCKS, 4)]
        assert len(GROUPS) <= 6

        block = ctx.enter_context(nc.Block())

        def flat(a):
            return a.rearrange("p s d -> p (s d)")

        def each(a):
            return a.unsqueeze(2).to_broadcast([a.shape[0], a.shape[1], D])

        def columns(k, first):
            return flat(edges[:, bass.ds(k * ROUND + first, TILES), :])

        def more_rounds(engine):
            engine.wait_ge(rounds_set, 1)
            return engine.value_load(rounds_i[0:1, 0:1], min_val=0, max_val=MOST - LEAST)

        @block.sync
        def _(sp):
            sp.wait_ge(padded, 3)
            for raw, first in ((s_raw, src), (d_raw, dst)):
                for lo, hi in ((0, 112), (112, P - 1)):
                    sp.dma_start(raw[lo:hi, :], first[lo * COLS:hi * COLS].rearrange("(p n) -> p n", n=COLS)
                                 ).then_inc(lists_in, 16)
                sp.dma_start(raw[P - 1:P, 0:LAST], first[(P - 1) * COLS:E][None, :]).then_inc(lists_in, 16)
            for lo, hi in ((0, 112), (112, P - 1)):
                sp.dma_start(d_next[lo:hi, :], dst[lo * COLS + 1:hi * COLS + 1].rearrange("(p n) -> p n", n=COLS)
                             ).then_inc(lists_in, 16)
            sp.dma_start(d_next[P - 1:P, 0:LAST - 1], dst[(P - 1) * COLS + 1:E][None, :]).then_inc(lists_in, 16)

            def fill(i, what):
                for c in range(NF):
                    sp.dma_start(acc[i][c * P * FILL:(c + 1) * P * FILL, :].rearrange("(p r) d -> p r d", p=P),
                                 what[:]).then_inc(filled, 16)
                sp.dma_start(acc[i][NF * P * FILL:N, :].rearrange("(p r) d -> p r d", p=REST_P),
                             what[0:REST_P, 0:REST_R]).then_inc(filled, 16)

            sp.wait_ge(zeroed, 1)
            fill(1, zero_fill)
            sp.wait_ge(setup, FILL_MADE)
            fill(0, b2_fill)

            def load_ends(u, first_row):
                sp.dma_start(flat(ends[u][:]),
                             tile_rows[bass.ds(first_row, SLOTS), :].rearrange("s q -> (s q)").partition_broadcast(P)
                             ).then_inc(ends_in[u], 16)

            def load_x(first):
                sp.dma_start(nx[:], x[bass.ds(first, CHUNK), :].rearrange("(p r) d -> p r d", p=P)).then_inc(n_in, 16)

            def sp_round(k, load, old):
                for u in range(2):
                    sp.wait_ge(same_set, k * 2 + (u + 1))
                    load_ends(u, k * (ROUND * ENDS) + (u + 2) * SLOTS)
                if load:
                    sp.wait_ge(n_xh_set, k + 1)
                    load_x(k * CHUNK + (CHUNK - OVER))
                if old:
                    sp.wait_ge(n_out_set, k)
                    sp.dma_start(dense[bass.ds(k * CHUNK - CHUNK, CHUNK), :].rearrange("(p r) d -> p r d", p=P),
                                 n_out[:]).then_inc(n_stored, 16)
                    sp.wait_ge(n_stored, k * 16)
                    sp.sem_inc(n_out_free, 1)

            sp.sem_inc(n_out_free, 1)
            load_x(0)
            sp.wait_ge(list_stored, 16 * len(GROUPS))
            for u in range(2):
                load_ends(u, u * SLOTS)
            more = more_rounds(sp)
            sp_round(0, True, False)
            with sp.Fori(1, NCH - 1) as k:
                sp_round(k, True, True)
            sp_round(NCH - 1, False, True)
            sp_round(NCH, False, True)
            with sp.Fori(NCH + 1, more + LEAST) as k:
                sp_round(k, False, False)

            sp.wait_ge(all_scattered, 1)

            def load_step(b, first):
                for to, whence, at in ((fs, acc[0], first), (fd, acc[1], first), (fn, dense, first + OVER)):
                    sp.dma_start(to[b][:], whence[bass.ds(at, FC * CHUNK), :].rearrange("(c p r) d -> p c r d", p=P, c=FC)
                                 ).then_inc(f_in[b], 16)

            for c in range(FC):
                start = c * CHUNK - OVER if c else 0
                for to, whence, at in ((fs, acc[0], start), (fd, acc[1], start), (fn, dense, c * CHUNK)):
                    sp.dma_start(to[0][:, c], whence[at:at + CHUNK, :].rearrange("(p r) d -> p r d", p=P)
                                 ).then_inc(f_in[0], 16)
            for t in range(1, FB):
                load_step(t, FC * t * CHUNK - OVER)
            with sp.Fori(1, STEPS // FB) as k:
                for b in range(FB):
                    sp.wait_ge(f_stored[b], k * 16 + (16 if b == 0 else 0))
                    load_step(b, k * (FC * FB * CHUNK) + (FC * b * CHUNK - OVER))
            sp.wait_ge(f_stored[0], 16 * (STEPS // FB + 1))
            load_step(0, FC * STEPS * CHUNK - OVER)

        @block.gpsimd
        def _(pool):
            nc.gpsimd.memset(zero_fill[:], 0.0).then_inc(zeroed, 1)
            nc.gpsimd.memset(ones[:], 1.0).then_inc(consts, 1)
            nc.gpsimd.memset(eps[:], EPS).then_inc(consts, 1)
            pool.wait_ge(consts, 1)
            nc.gpsimd.affine_select(out=ident[:], in_=ones[:], compare_op=ALU.is_equal, fill=0.0, base=0,
                                    pattern=[[-1, P]], channel_multiplier=1).then_inc(consts, 1)
            nc.gpsimd.affine_select(out=before[:], in_=ones[:], compare_op=ALU.is_gt, fill=0.0, base=0,
                                    pattern=[[-1, P]], channel_multiplier=1).then_inc(consts, 1)
            nc.gpsimd.iota(column[:], [[1, COLS]], base=0, channel_multiplier=0,
                           allow_small_or_imprecise_dtypes=True).then_inc(consts, 1)
            nc.gpsimd.iota(spare[:], [[0, 1]], base=N, channel_multiplier=1,
                           allow_small_or_imprecise_dtypes=True).then_inc(consts, 1)
            pool.wait_ge(zeroed, 1)
            for i in range(ENDS):
                pool.dma_start(acc[i][N:N + P, :], zero_fill[:, 0, :]).then_inc(added[i], 16)
            pool.sem_inc(scattered, 1)

            def gather(u, s):
                pool.indirect_dma_start(
                    out=rows[u][:, s, :], out_offset=None, in_=x[:, :],
                    in_offset=bass.IndirectOffsetOnAxis(ap=g_idx[u][:, s:s + 1], axis=0)).then_inc(gathered[u], 16)

            def scatter(u, s, done):
                pool.wait_ge(added[s % ENDS], done)
                pool.sem_inc(pool_steps, 1)
                pool.indirect_dma_start(
                    out=acc[s % ENDS][:, :],
                    out_offset=bass.IndirectOffsetOnAxis(ap=s_idx[u][:, s:s + 1], axis=0),
                    in_=upd[u][:, s, :], in_offset=None, compute_op=ALU.add).then_inc(added[s % ENDS], 16)

            def scatter_tile(u, t, k):
                if t == 0:
                    pool.wait_ge(e_upd_set, k * 2 + (u + 1))
                    pool.wait_ge(s_idx_set, k * 2 + (u + 1))
                    pool.sem_inc(pool_steps, 1)
                for end in range(ENDS):
                    scatter(u, ENDS * t + end, k * (16 * ROUND) + 16 * (u * TILES + t + 1))
                if t == 0:
                    pool.sem_inc(scattered, 1)

            more = more_rounds(pool)
            for i in range(3):
                pool.wait_ge(g_idx_set, i + 1)
                if i == 2:
                    pool.wait_ge(e_centred, 1)
                for s in range(SLOTS):
                    gather(i % 2, s)
            pool.wait_ge(filled, 16 * N_FILLS)
            with pool.Fori(0, more + (LEAST - 1)) as k:
                for u in range(2):
                    pool.wait_ge(g_idx_set, k * 2 + (u + 4))
                    pool.wait_ge(e_centred, k * 2 + (u + 2))
                    pool.sem_inc(pool_steps, 1)
                    for t in range(TILES):
                        for end in range(ENDS):
                            gather(1 - u, ENDS * t + end)
                        scatter_tile(u, t, k)
            for u in range(2):
                for t in range(TILES):
                    scatter_tile(u, t, more + (LEAST - 1))
            for i in range(ENDS):
                pool.wait_ge(added[i], more * (16 * ROUND) + 16 * (LEAST * ROUND + 1))
            pool.sem_inc(all_scattered, 1)

        @block.scalar
        def _(act):
            act.dma_start(w1[:], W1).then_inc(weights_in, 16)
            act.dma_start(w1x[0:D, :], W1[D:2 * D, :]).then_inc(weights_in, 16)
            act.dma_start(w1x[D:2 * D, :], W1[0:D, :]).then_inc(weights_in, 16)
            act.dma_start(w2[:], W2).then_inc(weights_in, 16)
            act.dma_start(b1c[:], b1[:, None]).then_inc(weights_in, 16)
            act.dma_start(b2r[:], b2.partition_broadcast(P)).then_inc(weights_in, 16)
            act.wait_ge(consts, ALL_CONSTS)
            nc.scalar.activation(root_of[:], eps[:], ACT.Sqrt).then_inc(root_table, 1)
            for n, group in enumerate(GROUPS):
                act.wait_ge(list_turned, n + 1)
                nc.scalar.copy(turned_list[:, group[0]:group[-1] + 1, :],
                               bank[n][:, 0:len(group) * P].rearrange("p (b q) -> p b q", q=P)).then_inc(list_copied, 1)
                act.wait_ge(list_copied, n + 1)
                act.dma_start(
                    tile_rows[group[0] * P:(group[-1] + 1) * P, :].rearrange("(b p) q -> p b q", p=P),
                    turned_list[:, group[0]:group[-1] + 1, :]).then_inc(list_stored, 16)
            act.wait_ge(weights_in, ALL_WEIGHTS)

            def square_pair(m):
                act.wait_ge(e_centred, m)
                nc.scalar.activation(e_sq[:], e_cen[:], ACT.Square).then_inc(e_squared, 1)

            def root_pair(m):
                act.wait_ge(e_var_set, m)
                nc.scalar.activation(e_std[:], e_var[:], ACT.Sqrt, bias=eps[:], scale=1.0 / D).then_inc(e_std_set, 1)

            def turn_pair(m):
                act.wait_ge(e_turned, m)
                nc.scalar.copy(e_hT[:], E_TURN[:, 0:TILES * P]).then_inc(e_hT_set, 1)

            def part_pair(which, whole, ready, n):
                act.wait_ge(ready, n)
                nc.scalar.copy(e_part[:, which], whole[:]).then_inc(e_part_set, 1)

            def act_slot(u, k, new):
                n, m = k * 2 + (u + 1), k * 2 + (u + 2)
                square_pair(m)
                root_pair(m)
                act.wait_ge(e_hid_made, n)
                nc.scalar.activation(e_hid[:].rearrange("p e t n -> p (e t n)"), E_HID[:], ACT.Relu,
                                     bias=b1c[:]).then_inc(e_hid_set, 1)
                if new and u == 1:
                    act.wait_ge(n_turned, k + 1)
                    nc.scalar.copy(n_hT[:], N_TURN[:]).then_inc(n_hT_set, 1)
                turn_pair(m)
                if new and u == 0:
                    act.wait_ge(n_centred, k + 1)
                    nc.scalar.activation(n_sq[:], n_cen[:], ACT.Square).then_inc(n_squared, 1)
                part_pair(0, e_msg, e_msg_set, n)
                if new and u == 0:
                    act.wait_ge(n_var_set, k + 1)
                    nc.scalar.activation(n_std[:], n_var[:], ACT.Sqrt, bias=eps[:], scale=1.0 / D
                                         ).then_inc(n_std_set, 1)
                for half in range(2):
                    if new and u == 1:
                        act.wait_ge(n_hid_made, k * 2 + (half + 1))
                        nc.scalar.activation(n_hid[:, half], N_HID[half][:], ACT.Relu, bias=b1c[:]
                                             ).then_inc(n_hid_set, 1)
                    if half == 0:
                        part_pair(1, e_rest, e_rest_set, n)
                act.wait_ge(scattered, n)
                act.wait_ge(e_upd_made, n)
                nc.scalar.copy(flat(upd[u][:]), E_UPD[:, 0:SLOTS * D]).then_inc(e_upd_set, 1)

            more = more_rounds(act)
            square_pair(1)
            root_pair(1)
            turn_pair(1)
            for u in range(2):
                act_slot(u, 0, True)
            with act.Fori(1, NCH) as k:
                for u in range(2):
                    act_slot(u, k, True)
            with act.Fori(NCH, more + LEAST) as k:
                for u in range(2):
                    act_slot(u, k, False)

            def store_step(b, first, count):
                act.wait_ge(f_out_set, count)
                act.dma_start(out[bass.ds(first, FC * CHUNK), :].rearrange("(c p r) d -> p c r d", p=P, c=FC),
                              fs[b][:]).then_inc(f_stored[b], 16)

            act.wait_ge(f_out_set, 1)
            act.dma_start(out[0:CHUNK, :].rearrange("(p r) d -> p r d", p=P), fs[0][:, 0]).then_inc(f_stored[0], 16)
            act.wait_ge(f_stored[0], 16)
            act.dma_start(out[CHUNK - OVER:2 * CHUNK - OVER, :].rearrange("(p r) d -> p r d", p=P), fs[0][:, 1]
                          ).then_inc(f_stored[0], 16)
            for t in range(1, FB):
                store_step(t, FC * t * CHUNK - OVER, t + 1)
            with act.Fori(1, STEPS // FB) as k:
                for b in range(FB):
                    store_step(b, k * (FC * FB * CHUNK) + (FC * b * CHUNK - OVER), k * FB + (b + 1))
            store_step(0, FC * STEPS * CHUNK - OVER, STEPS + 1)
            for b in range(FB):
                act.wait_ge(f_stored[b], 16 * (STEPS // FB + (2 if b == 0 else 0)))

        @block.vector
        def _(dve):
            count = [0]

            def step(ins):
                count[0] += 1
                ins.then_inc(setup, 1)
                dve.wait_ge(setup, count[0])

            nc.vector.memset(s_raw[:], -1).then_inc(padded, 1)
            nc.vector.memset(d_raw[:], -1).then_inc(padded, 1)
            nc.vector.memset(d_next[:], FAR).then_inc(padded, 1)
            dve.wait_ge(lists_in, 16 * 9)
            step(nc.vector.tensor_tensor(loop_e[:], s_raw[:], d_raw[:], ALU.is_equal))
            step(nc.vector.tensor_tensor(drop[:], d_raw[:], d_next[:], ALU.not_equal))
            step(nc.vector.tensor_tensor(loop_e[:], loop_e[:], drop[:], ALU.mult))
            step(nc.vector.scalar_tensor_tensor(out=loop_e[:], in0=s_raw[:], scalar=0.0, in1=loop_e[:],
                                                op0=ALU.is_ge, op1=ALU.mult))
            step(nc.vector.tensor_tensor(keep[:], d_raw[:], d_next[:], ALU.is_gt))
            step(nc.vector.tensor_reduce(counts[:, 0:1], loop_e[:], AX.X, ALU.add))
            step(nc.vector.tensor_reduce(counts[:, 1:2], keep[:], AX.X, ALU.add))
            assert count[0] == COUNTED
            dve.wait_ge(sums, 1)
            step(nc.vector.tensor_scalar(flags[:, 0:1], bank[7][:, 0:1], float(N), None, ALU.is_equal))
            step(nc.vector.tensor_scalar(flags[:, 1:2], bank[7][:, 1:2], 0.0, None, ALU.is_equal))
            step(nc.vector.scalar_tensor_tensor(out=flags[:, 2:3], in0=flags[:, 0:1], scalar=2.0,
                                                in1=flags[:, 1:2], op0=ALU.mult, op1=ALU.mult))
            step(nc.vector.tensor_scalar(flags[:, 3:4], flags[:, 2:3], -0.5, None, ALU.mult))
            dve.wait_ge(weights_in, ALL_WEIGHTS)
            step(nc.vector.tensor_scalar(b2_fill[:], b2r[:].unsqueeze(1).to_broadcast([P, FILL, D]),
                                         flags[:, 2:3], None, ALU.mult))
            assert count[0] == FILL_MADE
            step(nc.vector.tensor_scalar(drop[:], s_raw[:], 0.0, None, ALU.is_ge))
            step(nc.vector.scalar_tensor_tensor(out=keep[:], in0=loop_e[:], scalar=flags[:, 3:4], in1=drop[:],
                                                op0=ALU.mult, op1=ALU.add))
            step(nc.vector.tensor_scalar(drop[:], keep[:], -1.0, 1.0, ALU.mult, ALU.add))
            step(nc.vector.tensor_reduce(kept[:], keep[:], AX.X, ALU.add))
            assert count[0] == KEPT
            step(nc.vector.tensor_tensor_scan(loop_e[:], drop[:], drop[:], 0.0, ALU.add, ALU.max))
            step(nc.vector.tensor_tensor(shift_i[:], loop_e[:], keep[:], ALU.mult))
            step(nc.vector.scalar_tensor_tensor(out=packed[:, 0], in0=s_raw[:], scalar=BITS, in1=shift_i[:],
                                                op0=ALU.logical_shift_left, op1=ALU.bitwise_or))
            for b in range(BITS):
                old, new, far = packed[:, b % 2], packed[:, (b + 1) % 2], 1 << b
                step(nc.vector.tensor_scalar(moves[:], old, 31 - b, 31, ALU.logical_shift_left,
                                             ALU.arith_shift_right))
                step(nc.vector.scalar_tensor_tensor(out=new, in0=moves[:], scalar=-1, in1=old,
                                                    op0=ALU.bitwise_xor, op1=ALU.bitwise_and))
                step(nc.vector.copy_predicated(new[:, 0:COLS - far], moves[:, far:], old[:, far:]))
                step(nc.vector.copy_predicated(d_raw[:, 0:COLS - far], moves[:, far:], d_raw[:, far:]))
            step(nc.vector.tensor_scalar(shift_i[:], packed[:, BITS % 2], BITS, None, ALU.arith_shift_right))
            step(nc.vector.tensor_copy(edges[:, 0:COLS, 0], shift_i[:]))
            step(nc.vector.tensor_copy(edges[:, 0:COLS, 1], d_raw[:]))
            step(nc.vector.tensor_copy(flat(edges[:, COLS:, :]), spare[:].to_broadcast([P, (WIDE - COLS) * ENDS])))
            step(nc.vector.tensor_scalar(moves[:], column[:], kept[:, 0:1], None, ALU.is_ge))
            for e in range(ENDS):
                step(nc.vector.copy_predicated(edges[:, 0:COLS, e], moves[:], spare[:].to_broadcast([P, COLS])))
            assert count[0] == LISTED
            dve.wait_ge(sums, 2)
            step(nc.vector.tensor_reduce(rounds_f[:, 0:1], bank[6][0:1, 0:P], AX.X, ALU.max))
            step(nc.vector.tensor_scalar(rounds_f[:, 1:2], rounds_f[:, 0:1], float(ROUND - 1 - LEAST * ROUND), 0.0,
                                         ALU.add, ALU.max))
            step(nc.vector.tensor_copy(rounds_i[:, 1:2], rounds_f[:, 1:2]))
            nc.vector.tensor_scalar(rounds_i[:, 0:1], rounds_i[:, 1:2], ROUND.bit_length() - 1, None,
                                    ALU.arith_shift_right).then_inc(rounds_set, 1)
            step(nc.vector.tensor_tensor(w1s[:], w1[:], w1x[:], ALU.add))
            assert count[0] == SETUP_DONE

            def prepare(u, cols):
                nc.vector.tensor_scalar(g_idx[u][:], cols, float(N - 1), None, ALU.min).then_inc(g_idx_set, 1)

            def centre_pair(u, m):
                nc.vector.tensor_reduce(e_sum[:], rows[u][:], AX.X, ALU.add).then_inc(e_summed, 1)
                dve.wait_ge(e_summed, m)
                nc.vector.scalar_tensor_tensor(out=e_cen[:], in0=each(e_sum[:]), scalar=-1.0 / D, in1=rows[u][:],
                                               op0=ALU.mult, op1=ALU.add).then_inc(e_centred, 1)

            def var_pair(m):
                dve.wait_ge(e_squared, m)
                nc.vector.tensor_reduce(e_var[:], e_sq[:], AX.X, ALU.add).then_inc(e_var_set, 1)

            def node_pair(m):
                dve.wait_ge(e_std_set, m)
                nc.vector.reciprocal(e_inv[:], e_std[:]).then_inc(e_inv_set, 1)
                dve.wait_ge(e_inv_set, m)
                nc.vector.scalar_tensor_tensor(out=e_h[:], in0=e_cen[:], scalar=0.0, in1=each(e_inv[:]),
                                               op0=ALU.max, op1=ALU.mult).then_inc(e_h_set, 1)

            def dve_slot(u, k, new, old):
                n, m = k * 2 + (u + 1), k * 2 + (u + 2)
                dve.wait_ge(gathered[1 - u], k * (16 * SLOTS) + 16 * SLOTS * (u + 1))
                centre_pair(1 - u, m)
                dve.wait_ge(ends_in[u], k * 16 + 16)
                nc.vector.tensor_tensor(same[u][:], ends[u][:],
                                        columns(k, u * TILES).unsqueeze(2).to_broadcast([P, SLOTS, P]),
                                        ALU.is_equal).then_inc(same_set, 1)
                var_pair(m)
                dve.wait_ge(same_set, n)
                nc.vector.tensor_tensor(same_b[:], same[u][:], before[:].unsqueeze(1).to_broadcast([P, SLOTS, P]),
                                        ALU.mult).then_inc(before_set, 1)
                dve.wait_ge(e_turned, n)
                node_pair(m)
                dve.wait_ge(before_set, n)
                nc.vector.tensor_reduce(dup[:], same_b[:], AX.X, ALU.add).then_inc(dup_set, 1)
                if new and u == 0:
                    dve.wait_ge(n_in, k * 16 + 16)
                    nc.vector.tensor_reduce(n_sum[:], nx[:], AX.X, ALU.add).then_inc(n_summed, 1)
                dve.wait_ge(dup_set, n)
                nc.vector.scalar_tensor_tensor(out=away[:], in0=dup[:], scalar=0.0,
                                               in1=spare[:].to_broadcast([P, SLOTS]),
                                               op0=ALU.is_gt, op1=ALU.mult).then_inc(away_set, 1)
                if new and u == 0:
                    dve.wait_ge(n_summed, k + 1)
                    nc.vector.scalar_tensor_tensor(out=n_cen[:], in0=each(n_sum[:]), scalar=-1.0 / D, in1=nx[:],
                                                   op0=ALU.mult, op1=ALU.add).then_inc(n_centred, 1)
                if old and u == 1:
                    dve.wait_ge(n_msg_made, k)
                    dve.wait_ge(n_out_free, k)
                    nc.vector.scalar_tensor_tensor(out=n_out[:], in0=N_MSG[:].rearrange("p (r d) -> p r d", r=R),
                                                   scalar=flags[:, 2:3], in1=n_xh[:], op0=ALU.mult,
                                                   op1=ALU.add).then_inc(n_out_set, 1)
                dve.wait_ge(away_set, n)
                dve.wait_ge(scattered, n)
                nc.vector.tensor_tensor(s_idx[u][:], columns(k, u * TILES), away[:], ALU.max).then_inc(s_idx_set, 1)
                prepare(1 - u, columns(k, (u + 3) * TILES))
                dve.wait_ge(e_msg_made, n)
                nc.vector.tensor_tensor(e_msg[:], E_MSG[:, 0:SLOTS * D].rearrange("p (s d) -> p s d", s=SLOTS),
                                        b2r[:].unsqueeze(1).to_broadcast([P, SLOTS, D]), ALU.add
                                        ).then_inc(e_msg_set, 1)
                if new and u == 0:
                    dve.wait_ge(n_squared, k + 1)
                    nc.vector.tensor_reduce(n_var[:], n_sq[:], AX.X, ALU.add).then_inc(n_var_set, 1)
                dve.wait_ge(e_msg_set, n)
                dve.wait_ge(e_part_set, k * 4 + (2 * u + 1))
                nc.vector.tensor_tensor(e_rest[:], e_msg[:], e_part[:, 0], ALU.subtract).then_inc(e_rest_set, 1)
                if new and u == 0:
                    dve.wait_ge(n_std_set, k + 1)
                    nc.vector.reciprocal(n_inv[:], n_std[:]).then_inc(n_inv_set, 1)
                    dve.wait_ge(n_inv_set, k + 1)
                    nc.vector.scalar_tensor_tensor(out=n_h[:], in0=n_cen[:], scalar=0.0, in1=each(n_inv[:]),
                                                   op0=ALU.max, op1=ALU.mult).then_inc(n_h_set, 1)
                if new and u == 1:
                    dve.wait_ge(n_h_set, k + 1)
                    nc.vector.tensor_tensor(n_xh[:], nx[:], n_h[:], ALU.add).then_inc(n_xh_set, 1)
                dve.wait_ge(e_rest_set, n)
                dve.wait_ge(e_part_set, k * 4 + (2 * u + 2))
                nc.vector.tensor_tensor(e_part[:, 2], e_rest[:], e_part[:, 1], ALU.subtract).then_inc(e_split_set, 1)

            more = more_rounds(dve)
            for i in range(3):
                if i == 2:
                    dve.wait_ge(gathered[0], 16 * SLOTS)
                    centre_pair(0, 1)
                prepare(i % 2, flat(edges[:, i * TILES:(i + 1) * TILES, :]))
            var_pair(1)
            node_pair(1)
            for u in range(2):
                dve_slot(u, 0, True, False)
            with dve.Fori(1, NCH) as k:
                for u in range(2):
                    dve_slot(u, k, True, True)
            for u in range(2):
                dve_slot(u, NCH, False, True)
            with dve.Fori(NCH + 1, more + LEAST) as k:
                for u in range(2):
                    dve_slot(u, k, False, False)

            def sum_step(b, landed, count):
                dve.wait_ge(f_in[b], landed)
                nc.vector.tensor_tensor(fs[b][:], fs[b][:], fd[b][:], ALU.add).then_inc(f_summed, 1)
                dve.wait_ge(f_summed, count)
                nc.vector.tensor_tensor(fs[b][:], fs[b][:], fn[b][:], ALU.add).then_inc(f_out_set, 1)

            for t in range(FB):
                sum_step(t, 96 if t == 0 else 48, t + 1)
            with dve.Fori(1, STEPS // FB) as k:
                for b in range(FB):
                    sum_step(b, k * 48 + (96 if b == 0 else 48), k * FB + (b + 1))
            sum_step(0, 48 * (STEPS // FB) + 96, STEPS + 1)

        @block.tensor
        def _(pe):
            pe.wait_ge(consts, ALL_CONSTS)
            pe.wait_ge(setup, COUNTED)
            nc.tensor.matmul(bank[7][:, 0:2], ones[:], counts[:], start=True, stop=True).then_inc(sums, 1)
            pe.wait_ge(setup, KEPT)
            nc.tensor.transpose(bank[6][0:1, 0:P], kept[:], ident[:]).then_inc(sums, 1)
            pe.wait_ge(setup, LISTED)
            for n, group in enumerate(GROUPS):
                for b in group:
                    last = nc.tensor.transpose(bank[n][:, (b % 4) * P:(b % 4 + 1) * P],
                                               flat(edges[:, b * P // ENDS:(b + 1) * P // ENDS, :]), ident[:])
                last.then_inc(list_turned, 1)
            pe.wait_ge(weights_in, ALL_WEIGHTS)
            pe.wait_ge(setup, SETUP_DONE)
            pe.wait_ge(list_copied, len(GROUPS))

            def turn_pair(m):
                pe.wait_ge(e_h_set, m)
                for t in range(TILES):
                    last = nc.tensor.transpose(E_TURN[:, t * P:(t + 1) * P],
                                               flat(e_h[:, ENDS * t:ENDS * (t + 1), :]), ident[:])
                last.then_inc(e_turned, 1)

            def turn_chunk(k):
                pe.wait_ge(n_h_set, k + 1)
                for r in range(R // 2):
                    last = nc.tensor.transpose(N_TURN[:, r * P:(r + 1) * P], flat(n_h[:, 2 * r:2 * r + 2, :]), ident[:])
                last.then_inc(n_turned, 1)

            def hidden_chunk(k):
                pe.wait_ge(n_hT_set, k + 1)
                for half in range(2):
                    part = slice(half * D, half * D + D)
                    nc.tensor.matmul(N_HID[half][:], w1s[part, :], n_hT[part, :], start=True, stop=True
                                     ).then_inc(n_hid_made, 1)

            def message_chunk(k, half):
                pe.wait_ge(n_hid_set, k * 2 + (half - 1))
                for r in range(R // 2):
                    o = (2 * r + half) * D
                    last = nc.tensor.matmul(N_MSG[:, o:o + D], n_hid[:, half, r * P:(r + 1) * P], w2[:],
                                            start=True, stop=True)
                if half == 1:
                    last.then_inc(n_msg_made, 1)

            def pe_slot(u, k, new, old):
                n, m = k * 2 + (u + 1), k * 2 + (u + 2)
                pe.wait_ge(e_hT_set, n)
                for end, w in enumerate((w1, w1x)):
                    last = nc.tensor.matmul(E_HID[:, end * TILES * P:(end + 1) * TILES * P], w[:], e_hT[:],
                                            start=True, stop=True)
                last.then_inc(e_hid_made, 1)
                if old and u == 0:
                    message_chunk(k, 0)
                if new and u == 1:
                    turn_chunk(k)
                turn_pair(m)
                pe.wait_ge(e_hid_set, n)
                for t in range(TILES):
                    for end in range(ENDS):
                        s = ENDS * t + end
                        last = nc.tensor.matmul(E_MSG[:, s * D:(s + 1) * D], e_hid[:, end, t, :], w2[:],
                                                start=True, stop=True)
                last.then_inc(e_msg_made, 1)
                if old and u == 0:
                    message_chunk(k, 1)
                if new and u == 1:
                    hidden_chunk(k)
                pe.wait_ge(e_split_set, n)
                pe.wait_ge(same_set, n)
                for s in range(SLOTS):
                    for part in range(PARTS):
                        last = nc.tensor.matmul(E_UPD[:, s * D:(s + 1) * D], same[u][:, s, :], e_part[:, part, s, :],
                                                start=(part == 0), stop=(part == PARTS - 1))
                last.then_inc(e_upd_made, 1)

            more = more_rounds(pe)
            turn_pair(1)
            for u in range(2):
                pe_slot(u, 0, True, False)
            with pe.Fori(1, NCH) as k:
                for u in range(2):
                    pe_slot(u, k, True, True)
            for u in range(2):
                pe_slot(u, NCH, False, True)
            with pe.Fori(NCH + 1, more + LEAST) as k:
                for u in range(2):
                    pe_slot(u, k, False, False)


_INS = ["x", "src", "dst", "L0_gnn_W1", "L0_gnn_b1", "L0_gnn_W2", "L0_gnn_b2"]


def kernel(**inputs):
    import numpy as _np
    import concourse.bacc as _bacc
    from concourse import mybir as _mybir
    from concourse.bass_utils import run_bass_kernel_spmd as _run

    nc = _bacc.Bacc("TRN2", target_bir_lowering=False, num_devices=1)
    arrays, args = {}, []
    for name in _INS:
        a = _np.ascontiguousarray(inputs[name])
        arrays[f"in_{name}_dram"] = a
        args.append(nc.dram_tensor(f"in_{name}_dram", a.shape, _mybir.dt.from_np(a.dtype), kind="ExternalInput").ap())
    out = nc.dram_tensor("out_dram", arrays["in_x_dram"].shape, _mybir.dt.float32, kind="ExternalOutput").ap()
    gnn_layer(nc, *args, out)
    r = _run(nc, [arrays], core_ids=[0])
    return r.results[0]["out_dram"]
```

```python
from contextlib import ExitStack

import concourse.bass as bass
from concourse import mybir

F32 = mybir.dt.float32
BF16 = mybir.dt.bfloat16
I32 = mybir.dt.int32
ALU = mybir.AluOpType
ACT = mybir.ActivationFunctionType
AX = mybir.AxisListType

P = 128
BANK = 512
ENDS = 2
TILES = 2
SLOTS = TILES * ENDS
PER_ROUND = 2
PARTS = 3
EPS = 1e-5
FAR = 1 << 23


def gnn_layer(
    nc: bass.Bass,
    x: bass.AP,
    src: bass.AP,
    dst: bass.AP,
    W1: bass.AP,
    b1: bass.AP,
    W2: bass.AP,
    b2: bass.AP,
    out: bass.AP,
):
    N, D = x.shape
    E = src.shape[0]
    H = W1.shape[1]
    assert H == P and 2 * D == P
    ROUND = PER_ROUND * TILES
    COLS = -(-E // P)
    COLS += -COLS % ROUND
    LAST = E - (P - 1) * COLS
    assert 1 < LAST <= COLS
    PAD_FROM = 96
    BITS = COLS.bit_length()
    assert N << BITS < 1 << 31
    BLOCKS = -(-(COLS + 4 * TILES) * ENDS // P)
    WIDE = BLOCKS * P // ENDS
    R = 8
    CHUNK = P * R
    NCH = -(-N // CHUNK)
    NCH += NCH % 2
    OVER = NCH * CHUNK - N
    assert 0 <= OVER <= CHUNK
    HELD = 60
    LEAST = NCH + 2
    AHEAD = 2 * PER_ROUND
    MOST = COLS // ROUND
    assert LEAST < MOST
    SPREAD = 2 * ROUND
    TAIL = LEAST * ROUND - SPREAD
    TAIL_W = WIDE - TAIL
    TAIL_BLOCK = TAIL * ENDS // P
    assert (TAIL + SPREAD) * ENDS <= (TAIL_BLOCK + 1) * P and P * TAIL_W < 1 << 24
    FILL = 25
    NF = N // (P * FILL)
    REST = N - NF * P * FILL
    REST_P = 32
    REST_R = REST // REST_P
    assert REST_P * REST_R == REST and REST_R <= FILL
    FC = 2
    FB = 3
    STEPS = (NCH - FC) // FC
    assert STEPS % FB == 0 and NCH % FC == 0 and HELD % (FC * FB) == 0 and HELD < NCH
    HELD_TURNS = HELD // (FC * FB)

    acc = nc.dram_tensor("accumulator", [N + ENDS * P, D], F32).ap()
    dense = nc.dram_tensor("dense", [(NCH - HELD) * CHUNK, D], F32).ap()
    tile_rows = nc.dram_tensor("tile_rows", [WIDE * ENDS, P], F32).ap()
    tail_rows = nc.dram_tensor("tail_rows", [P * TAIL_W, ENDS], F32).ap()

    with ExitStack() as ctx:
        def sb(name, shape, dt=F32):
            return ctx.enter_context(nc.sbuf_tensor(name, shape, dt))

        def sem(name):
            return ctx.enter_context(nc.semaphore(name))

        held = sb("held", [P, HELD * R * D])
        taken = [0]

        def early(columns, dt=F32):
            first = taken[0]
            taken[0] += columns
            assert taken[0] <= HELD * R * D
            piece = held[:, first:first + columns]
            return piece if dt == F32 else piece.bitcast(dt)

        WORK = max(R * D * 6 + BANK * 3 + BLOCKS * P, 2 * FB * FC * R * D)
        work = sb("work", [P, WORK])
        work_taken = [0]

        def work_piece(columns):
            first = work_taken[0]
            work_taken[0] += columns
            assert work_taken[0] <= WORK
            return work[:, first:first + columns]

        ident = sb("ident", [P, P])
        ones = sb("ones", [P, P])
        before = sb("before", [P, P], BF16)
        spare = sb("spare", [P, SLOTS])
        column = early(COLS)
        eps = sb("eps", [P, 1])
        root_of = sb("root_of", [P, 1])
        w1 = sb("w1", [P, H])
        w1x = sb("w1x", [P, H])
        w1s = sb("w1s", [P, H])
        w2 = sb("w2", [P, D])
        b1c = sb("b1c", [P, 1])
        b2r = sb("b2r", [P, D])
        b2_part = sb("b2_part", [P, PARTS, D], BF16)
        b2_rest = sb("b2_rest", [P, D])
        b2_own = sb("b2_own", [P, D])
        b2s = sb("b2s", [P, R, D], BF16)
        ones_b = sb("ones_b", [P, P], BF16)
        s_raw = early(COLS, I32)
        d_raw = early(COLS, I32)
        d_next = early(COLS, I32)
        loop_e = early(COLS)
        drop = early(COLS)
        ahead_n = early(COLS)
        shift_i = early(COLS, I32)
        packed = early(2 * COLS, I32).rearrange("p (b n) -> p b n", b=2)
        moves = early(COLS, I32)
        edges = sb("edges", [P, WIDE, ENDS])
        turned_list = work_piece(BLOCKS * P).rearrange("p (b q) -> p b q", q=P)
        counts = sb("counts", [P, 2])
        kept = sb("kept", [P, 1])
        flags = sb("flags", [P, 5])
        whole_n = sb("whole_n", [P, 1])
        in_list = sb("in_list", [P, 1])
        d_first = sb("d_first", [P, 1])
        zeros = sb("zeros", [P, ENDS, D])
        zero_fill = early(FILL * D).rearrange("p (r d) -> p r d", d=D)
        rounds_f = sb("rounds_f", [1, 2])
        rounds_i = sb("rounds_i", [1, 2], I32)
        rank = sb("rank", [P, SPREAD])
        stay = sb("stay", [P, SPREAD])
        none = sb("none", [P, 1])
        tail_n = sb("tail_n", [P, P])
        upto = sb("upto", [P, P])
        tail_end = sb("tail_end", [P, P])
        ended = early(SPREAD * P).rearrange("p (c q) -> p c q", q=P)
        ended_at = early(SPREAD * P).rearrange("p (c q) -> p c q", q=P)
        whose = sb("whose", [P, SPREAD])
        its_first = sb("its_first", [P, SPREAD])
        row = sb("row", [P, SPREAD])
        row_is = sb("row_is", [P, SPREAD])
        fits = sb("fits", [P, 1])
        row_i = sb("row_i", [P, SPREAD], I32)
        g_idx = [sb(f"g_idx{u}", [P, SLOTS], I32) for u in range(2)]
        s_idx = [sb(f"s_idx{u}", [P, SLOTS], I32) for u in range(2)]
        rows = [sb(f"rows{u}", [P, SLOTS, D]) for u in range(2)]
        upd = [sb(f"upd{u}", [P, SLOTS, D]) for u in range(2)]
        ends = [sb(f"ends{u}", [P, SLOTS, P]) for u in range(2)]
        same = [sb(f"same{u}", [P, SLOTS, P], BF16) for u in range(2)]
        seen = [sb(f"seen{u}", [P, TILES, 3, P], BF16) for u in range(2)]
        dup = sb("dup", [P, SLOTS])
        away = sb("away", [P, SLOTS])
        goal = [sb(f"goal{u}", [P, SLOTS]) for u in range(2)]
        e_sum = sb("e_sum", [P, SLOTS])
        e_cen = sb("e_cen", [P, SLOTS, D])
        e_sq = sb("e_sq", [P, SLOTS, D])
        e_var = sb("e_var", [P, SLOTS])
        e_std = sb("e_std", [P, SLOTS])
        e_inv = sb("e_inv", [P, SLOTS])
        e_h = sb("e_h", [P, SLOTS, D])
        e_hT = sb("e_hT", [P, TILES * P])
        e_hid = sb("e_hid", [P, ENDS, TILES, P])
        e_rest = sb("e_rest", [P, SLOTS, D])
        e_part = sb("e_part", [P, PARTS, SLOTS, D], BF16)
        nx = work_piece(R * D).rearrange("p (r d) -> p r d", d=D)
        n_sum = sb("n_sum", [P, R])
        n_cen = work_piece(R * D).rearrange("p (r d) -> p r d", d=D)
        n_sq = work_piece(R * D).rearrange("p (r d) -> p r d", d=D)
        n_var = sb("n_var", [P, R])
        n_std = sb("n_std", [P, R])
        n_inv = sb("n_inv", [P, R])
        n_h = work_piece(R * D).rearrange("p (r d) -> p r d", d=D)
        n_xh = work_piece(R * D).rearrange("p (r d) -> p r d", d=D)
        n_hT = work_piece(BANK)
        n_hid = work_piece(2 * BANK).rearrange("p (h n) -> p h n", h=2)
        n_out = work_piece(R * D).rearrange("p (r d) -> p r d", d=D)
        work_taken[0] = 0
        fs = [work_piece(FC * R * D).rearrange("p (c r d) -> p c r d", c=FC, d=D) for _ in range(FB)]
        fn = [work_piece(FC * R * D).rearrange("p (c r d) -> p c r d", c=FC, d=D) for _ in range(FB)]
        bank = [ctx.enter_context(nc.psum_tensor(f"bank{b}", [P, BANK], F32)) for b in range(8)]
        E_TURN, E_HID, E_MSG, E_UPD, N_TURN, N_HID, N_MSG = bank[0], bank[1], bank[2], bank[3], bank[4], bank[5:7], bank[7]

        padded = sem("padded")
        lists_in = sem("lists_in")
        next_in = sem("next_in")
        weights_in = sem("weights_in")
        consts = sem("consts")
        zeroed = sem("zeroed")
        sums = sem("sums")
        setup = sem("setup")
        list_turned = sem("list_turned")
        list_copied = sem("list_copied")
        list_stored = sem("list_stored")
        tail_summed = sem("tail_summed")
        tail_steps = sem("tail_steps")
        tail_idx_set = sem("tail_idx_set")
        b2_steps = sem("b2_steps")
        tail_stored = sem("tail_stored")
        tail_in = sem("tail_in")
        tail_turned = sem("tail_turned")
        tail_copied = sem("tail_copied")
        filled = sem("filled")
        rounds_set = sem("rounds_set")
        root_table = sem("root_table")
        whole_set = sem("whole_set")
        g_idx_set = sem("g_idx_set")
        gathered = [sem(f"gathered{u}") for u in range(2)]
        added = [sem(f"added_{n}") for n in ("src", "dst")]
        pool_steps = sem("pool_steps")
        scattered = sem("scattered")
        all_scattered = sem("all_scattered")
        ends_in = [sem(f"ends_in{u}") for u in range(2)]
        same_set = sem("same_set")
        seen_set = sem("seen_set")
        dup_set = sem("dup_set")
        away_set = sem("away_set")
        goal_set = sem("goal_set")
        s_idx_set = sem("s_idx_set")
        e_summed = sem("e_summed")
        e_centred = sem("e_centred")
        e_squared = sem("e_squared")
        e_var_set = sem("e_var_set")
        e_std_set = sem("e_std_set")
        e_inv_set = sem("e_inv_set")
        e_h_set = sem("e_h_set")
        e_turned = sem("e_turned")
        e_hT_set = sem("e_hT_set")
        e_hid_made = sem("e_hid_made")
        e_hid_set = sem("e_hid_set")
        e_msg_made = sem("e_msg_made")
        e_part_set = sem("e_part_set")
        e_rest_set = sem("e_rest_set")
        e_split_set = sem("e_split_set")
        e_upd_made = sem("e_upd_made")
        e_upd_set = sem("e_upd_set")
        n_in = sem("n_in")
        n_summed = sem("n_summed")
        n_centred = sem("n_centred")
        n_squared = sem("n_squared")
        n_var_set = sem("n_var_set")
        n_std_set = sem("n_std_set")
        n_inv_set = sem("n_inv_set")
        n_h_set = sem("n_h_set")
        n_xh_set = sem("n_xh_set")
        n_turned = sem("n_turned")
        n_hT_set = sem("n_hT_set")
        n_hid_made = sem("n_hid_made")
        n_hid_set = sem("n_hid_set")
        n_msg_made = sem("n_msg_made")
        n_out_set = sem("n_out_set")
        n_stored = sem("n_stored")
        n_out_free = sem("n_out_free")
        f_in = [sem(f"f_in{b}") for b in range(FB)]
        f_stored = [sem(f"f_stored{b}") for b in range(FB)]
        f_out_set = sem("f_out_set")

        COUNTED = 6
        KEPT = COUNTED + 9
        B2_DONE = 6 + PARTS
        LISTED = KEPT + 3 + 3 * BITS + 10
        SETUP_DONE = LISTED + 4 + 1
        N_FILLS = NF + 1
        ALL_WEIGHTS = 16 * 6
        ALL_CONSTS = 10
        GROUPS = [list(range(b, min(b + 4, BLOCKS))) for b in range(0, BLOCKS, 4)]
        assert len(GROUPS) <= 6

        block = ctx.enter_context(nc.Block())

        def flat(a):
            return a.rearrange("p s d -> p (s d)")

        def each(a):
            return a.unsqueeze(2).to_broadcast([a.shape[0], a.shape[1], D])

        def columns(k, first):
            return flat(edges[:, bass.ds(k * ROUND + first, TILES), :])

        def by_tile(a):
            return a[:].rearrange("p (t e) q -> p t e q", e=ENDS)

        def by_tile_column(k, first):
            return edges[:, bass.ds(k * ROUND + first, TILES), :]

        def by_end(a, end):
            return a[:].rearrange("p (t e) -> p t e", e=ENDS)[:, :, end]

        def held_chunks(first, chunks):
            return held[:].rearrange("p (c r d) -> p c r d", r=R, d=D)[:, bass.ds(first, chunks)]

        def messages():
            return E_MSG[:, 0:SLOTS * D].rearrange("p (s d) -> p s d", s=SLOTS)

        def more_rounds(engine):
            engine.wait_ge(rounds_set, 1)
            return engine.value_load(rounds_i[0:1, 0:1], min_val=0, max_val=MOST - LEAST)

        @block.sync
        def _(sp):
            sp.wait_ge(padded, 3)
            for raw, first in ((s_raw, src), (d_raw, dst)):
                for lo, hi in ((0, 112), (112, P - 1)):
                    sp.dma_start(raw[lo:hi, :], first[lo * COLS:hi * COLS].rearrange("(p n) -> p n", n=COLS)
                                 ).then_inc(lists_in, 16)
                sp.dma_start(raw[P - 1:P, 0:LAST], first[(P - 1) * COLS:E][None, :]).then_inc(lists_in, 16)
            for lo, hi in ((0, 112), (112, P - 1)):
                sp.dma_start(d_next[lo:hi, :], dst[lo * COLS + 1:hi * COLS + 1].rearrange("(p n) -> p n", n=COLS)
                             ).then_inc(next_in, 16)
            sp.dma_start(d_next[P - 1:P, 0:LAST - 1], dst[(P - 1) * COLS + 1:E][None, :]).then_inc(next_in, 16)

            sp.wait_ge(zeroed, 2)
            for c in range(NF):
                sp.dma_start(acc[c * P * FILL:(c + 1) * P * FILL, :].rearrange("(p r) d -> p r d", p=P),
                             zero_fill[:]).then_inc(filled, 16)
            sp.dma_start(acc[NF * P * FILL:N, :].rearrange("(p r) d -> p r d", p=REST_P),
                         zero_fill[0:REST_P, 0:REST_R]).then_inc(filled, 16)

            sp.wait_ge(setup, LISTED)
            sp.dma_start(tail_rows.rearrange("(p n) e -> p n e", p=P), edges[:, TAIL:, :]).then_inc(tail_stored, 16)

            def load_ends(u, first_row):
                sp.dma_start(flat(ends[u][:]),
                             tile_rows[bass.ds(first_row, SLOTS), :].rearrange("s q -> (s q)").partition_broadcast(P)
                             ).then_inc(ends_in[u], 16)

            def load_x(first):
                sp.dma_start(nx[:], x[bass.ds(first, CHUNK), :].rearrange("(p r) d -> p r d", p=P)).then_inc(n_in, 16)

            def sp_round(k, load, store):
                for u in range(2):
                    sp.wait_ge(same_set, k * 2 + (u + 1))
                    load_ends(u, k * (ROUND * ENDS) + (u + 2) * SLOTS)
                if store:
                    sp.wait_ge(n_out_set, k)
                    sp.dma_start(dense[bass.ds(k * CHUNK - (HELD + 1) * CHUNK, CHUNK), :].rearrange("(p r) d -> p r d", p=P),
                                 n_out[:]).then_inc(n_stored, 16)
                if load:
                    sp.wait_ge(n_xh_set, k + 1)
                    load_x(k * CHUNK + (CHUNK - OVER))
                if store:
                    sp.wait_ge(n_stored, k * 16 - HELD * 16)
                    sp.sem_inc(n_out_free, 1)

            sp.sem_inc(n_out_free, 1)
            load_x(0)
            sp.wait_ge(list_stored, 16 * len(GROUPS))
            for u in range(2):
                load_ends(u, u * SLOTS)
            more = more_rounds(sp)
            sp_round(0, True, False)
            sp.wait_ge(list_stored, 16 * (len(GROUPS) + 1))
            with sp.Fori(1, HELD + 1) as k:
                sp_round(k, True, False)
            with sp.Fori(HELD + 1, NCH - 1) as k:
                sp_round(k, True, True)
            sp_round(NCH - 1, False, True)
            sp_round(NCH, False, True)
            with sp.Fori(NCH + 1, more + LEAST) as k:
                sp_round(k, False, False)

            sp.wait_ge(all_scattered, 1)

            def load_step(b, first, stored):
                places = [(fs, acc, first)]
                if stored:
                    places.append((fn, dense, first + (OVER - HELD * CHUNK)))
                for to, whence, at in places:
                    sp.dma_start(to[b][:], whence[bass.ds(at, FC * CHUNK), :].rearrange("(c p r) d -> p c r d", p=P, c=FC)
                                 ).then_inc(f_in[b], 16)

            for c in range(FC):
                start = c * CHUNK - OVER if c else 0
                sp.dma_start(fs[0][:, c], acc[start:start + CHUNK, :].rearrange("(p r) d -> p r d", p=P)
                             ).then_inc(f_in[0], 16)
            for t in range(1, FB):
                load_step(t, FC * t * CHUNK - OVER, False)
            for first_turn, last_turn, stored in ((1, HELD_TURNS, False), (HELD_TURNS, STEPS // FB, True)):
                with sp.Fori(first_turn, last_turn) as k:
                    for b in range(FB):
                        sp.wait_ge(f_stored[b], k * 16 + (16 if b == 0 else 0))
                        load_step(b, k * (FC * FB * CHUNK) + (FC * b * CHUNK - OVER), stored)
            sp.wait_ge(f_stored[0], 16 * (STEPS // FB + 1))
            load_step(0, FC * STEPS * CHUNK - OVER, True)

        @block.gpsimd
        def _(pool):
            nc.gpsimd.memset(zeros[:], 0.0).then_inc(zeroed, 1)
            nc.gpsimd.memset(zero_fill[:], 0.0).then_inc(zeroed, 1)
            nc.gpsimd.memset(ones[:], 1.0).then_inc(consts, 1)
            nc.gpsimd.memset(eps[:], EPS).then_inc(consts, 1)
            pool.wait_ge(consts, 1)
            nc.gpsimd.affine_select(out=ident[:], in_=ones[:], compare_op=ALU.is_equal, fill=0.0, base=0,
                                    pattern=[[-1, P]], channel_multiplier=1).then_inc(consts, 1)
            nc.gpsimd.affine_select(out=before[:], in_=ones[:], compare_op=ALU.is_gt, fill=0.0, base=0,
                                    pattern=[[-1, P]], channel_multiplier=1).then_inc(consts, 1)
            nc.gpsimd.iota(column[:], [[1, COLS]], base=0, channel_multiplier=0,
                           allow_small_or_imprecise_dtypes=True).then_inc(consts, 1)
            nc.gpsimd.iota(spare[:], [[0, TILES], [P, ENDS]], base=N, channel_multiplier=1,
                           allow_small_or_imprecise_dtypes=True).then_inc(consts, 1)
            nc.gpsimd.iota(rank[:], [[P, SPREAD]], base=0, channel_multiplier=1,
                           allow_small_or_imprecise_dtypes=True).then_inc(consts, 1)
            nc.gpsimd.iota(stay[:], [[1, SPREAD]], base=0, channel_multiplier=TAIL_W,
                           allow_small_or_imprecise_dtypes=True).then_inc(consts, 1)
            nc.gpsimd.iota(none[:], [[0, 1]], base=TAIL_W - 1, channel_multiplier=TAIL_W,
                           allow_small_or_imprecise_dtypes=True).then_inc(consts, 1)
            nc.gpsimd.memset(whole_n[:], float(COLS)).then_inc(whole_set, 1)
            pool.wait_ge(whole_set, 1)
            nc.gpsimd.affine_select(out=in_list[:], in_=whole_n[:], compare_op=ALU.is_gt, fill=float(LAST), base=P - 1,
                                    pattern=[[0, 1]], channel_multiplier=-1).then_inc(consts, 1)
            pool.wait_ge(zeroed, 1)
            for end in range(ENDS):
                pool.dma_start(acc[N + end * P:N + (end + 1) * P, :], zeros[:, end, :]).then_inc(added[end], 16)
            pool.sem_inc(scattered, 1)

            def gather(u, s):
                pool.indirect_dma_start(
                    out=rows[u][:, s, :], out_offset=None, in_=x[:, :],
                    in_offset=bass.IndirectOffsetOnAxis(ap=g_idx[u][:, s:s + 1], axis=0)).then_inc(gathered[u], 16)

            def scatter_tile(u, t, k):
                if t == 0:
                    pool.wait_ge(e_upd_set, k * 2 + (u + 1))
                    pool.wait_ge(s_idx_set, k * 2 + (u + 1))
                    pool.sem_inc(pool_steps, 1)
                done = k * (16 * ROUND) + 16 * (u * TILES + t + 1)
                for end in range(ENDS):
                    pool.wait_ge(added[end], done)
                pool.sem_inc(scattered if t == 0 else pool_steps, 1)
                for end in range(ENDS):
                    s = ENDS * t + end
                    pool.indirect_dma_start(
                        out=acc[:, :], out_offset=bass.IndirectOffsetOnAxis(ap=s_idx[u][:, s:s + 1], axis=0),
                        in_=upd[u][:, s, :], in_offset=None, compute_op=ALU.add).then_inc(added[end], 16)

            more = more_rounds(pool)
            for i in range(AHEAD):
                pool.wait_ge(g_idx_set, i + 1)
                if i >= 2:
                    pool.wait_ge(e_centred, i - 1)
                for s in range(SLOTS):
                    gather(i % 2, s)
                if i == 1:
                    pool.wait_ge(tail_idx_set, 1)
                    pool.wait_ge(tail_stored, 16)
                    pool.wait_ge(list_turned, len(GROUPS))
                    pool.sem_inc(pool_steps, 1)
                    for c in range(SPREAD):
                        pool.indirect_dma_start(
                            out=edges[:, TAIL + c, :], out_offset=None, in_=tail_rows[:, :],
                            in_offset=bass.IndirectOffsetOnAxis(ap=row_i[:, c:c + 1], axis=0)).then_inc(tail_in, 16)
            pool.wait_ge(filled, 16 * N_FILLS)

            def pool_pair(u, k, load=True):
                if load:
                    pool.wait_ge(g_idx_set, k * 2 + (u + AHEAD + 1))
                    pool.wait_ge(e_centred, k * 2 + (u + AHEAD - 1))
                    pool.sem_inc(pool_steps, 1)
                for t in range(TILES):
                    if load:
                        for end in range(ENDS):
                            gather(u, ENDS * t + end)
                    scatter_tile(u, t, k)

            with pool.Fori(0, more + (LEAST - AHEAD // PER_ROUND)) as k:
                for u in range(2):
                    pool_pair(u, k)
            for k in range(LEAST - AHEAD // PER_ROUND, LEAST):
                for u in range(2):
                    pool_pair(u, more + k, load=(k * PER_ROUND + u + AHEAD == LEAST * PER_ROUND))
            for i in range(ENDS):
                pool.wait_ge(added[i], more * (16 * ROUND) + 16 * (LEAST * ROUND + 1))
            pool.sem_inc(all_scattered, 1)

        @block.scalar
        def _(act):
            act.dma_start(w1[:], W1).then_inc(weights_in, 16)
            act.dma_start(w1x[0:D, :], W1[D:2 * D, :]).then_inc(weights_in, 16)
            act.dma_start(w1x[D:2 * D, :], W1[0:D, :]).then_inc(weights_in, 16)
            act.dma_start(w2[:], W2).then_inc(weights_in, 16)
            act.dma_start(b1c[:], b1[:, None]).then_inc(weights_in, 16)
            act.dma_start(b2r[:], b2.partition_broadcast(P)).then_inc(weights_in, 16)
            act.wait_ge(consts, ALL_CONSTS)
            nc.scalar.activation(root_of[:], eps[:], ACT.Sqrt).then_inc(root_table, 1)
            for n, group in enumerate(GROUPS):
                act.wait_ge(list_turned, n + 1)
                nc.scalar.copy(turned_list[:, group[0]:group[-1] + 1, :],
                               bank[n][:, 0:len(group) * P].rearrange("p (b q) -> p b q", q=P)).then_inc(list_copied, 1)
                act.wait_ge(list_copied, n + 1)
                act.dma_start(
                    tile_rows[group[0] * P:(group[-1] + 1) * P, :].rearrange("(b p) q -> p b q", p=P),
                    turned_list[:, group[0]:group[-1] + 1, :]).then_inc(list_stored, 16)
            act.wait_ge(weights_in, ALL_WEIGHTS)

            def square_pair(m):
                act.wait_ge(e_centred, m)
                nc.scalar.activation(e_sq[:], e_cen[:], ACT.Square).then_inc(e_squared, 1)

            def root_pair(m):
                act.wait_ge(e_var_set, m)
                nc.scalar.activation(e_std[:], e_var[:], ACT.Sqrt, bias=eps[:], scale=1.0 / D).then_inc(e_std_set, 1)

            def turn_pair(m):
                act.wait_ge(e_turned, m)
                nc.scalar.copy(e_hT[:], E_TURN[:, 0:TILES * P]).then_inc(e_hT_set, 1)

            def part_pair(which, whole, ready, n):
                act.wait_ge(ready, n)
                nc.scalar.copy(e_part[:, which], whole).then_inc(e_part_set, 1)

            def sum_pair(v, m):
                act.wait_ge(scattered, m)
                act.wait_ge(e_upd_made, m)
                nc.scalar.copy(flat(upd[v][:]), E_UPD[:, 0:SLOTS * D]).then_inc(e_upd_set, 1)

            def act_slot(u, k, new, first=False):
                n, m = k * 2 + (u + 1), k * 2 + (u + 2)
                square_pair(m)
                root_pair(m)
                act.wait_ge(e_hid_made, n)
                nc.scalar.activation(e_hid[:].rearrange("p e t n -> p (e t n)"), E_HID[:], ACT.Relu,
                                     bias=b1c[:]).then_inc(e_hid_set, 1)
                if not first:
                    sum_pair(1 - u, k * 2 + u)
                turn_pair(m)
                if new and u == 1:
                    act.wait_ge(n_turned, k + 1)
                    nc.scalar.copy(n_hT[:], N_TURN[:]).then_inc(n_hT_set, 1)
                if new and u == 0:
                    act.wait_ge(n_centred, k + 1)
                    nc.scalar.activation(n_sq[:], n_cen[:], ACT.Square).then_inc(n_squared, 1)
                part_pair(0, messages(), e_msg_made, n)
                if new and u == 0:
                    act.wait_ge(n_var_set, k + 1)
                    nc.scalar.activation(n_std[:], n_var[:], ACT.Sqrt, bias=eps[:], scale=1.0 / D
                                         ).then_inc(n_std_set, 1)
                part_pair(1, e_rest[:], e_rest_set, n)
                if new and u == 1:
                    for half in range(2):
                        act.wait_ge(n_hid_made, k * 2 + (half + 1))
                        nc.scalar.activation(n_hid[:, half], N_HID[half][:], ACT.Relu, bias=b1c[:]
                                             ).then_inc(n_hid_set, 1)

            more = more_rounds(act)
            square_pair(1)
            root_pair(1)
            turn_pair(1)
            for u in range(2):
                act_slot(u, 0, True, first=(u == 0))
            act.wait_ge(tail_turned, 1)
            act.wait_ge(list_stored, 16 * len(GROUPS))
            nc.scalar.copy(turned_list[:, TAIL_BLOCK, :], E_TURN[:, TILES * P:(TILES + 1) * P]).then_inc(tail_copied, 1)
            act.wait_ge(tail_copied, 1)
            act.dma_start(tile_rows[TAIL_BLOCK * P:(TAIL_BLOCK + 1) * P, :], turned_list[:, TAIL_BLOCK, :]
                          ).then_inc(list_stored, 16)
            with act.Fori(1, NCH) as k:
                for u in range(2):
                    act_slot(u, k, True)
            with act.Fori(NCH, more + LEAST) as k:
                for u in range(2):
                    act_slot(u, k, False)
            sum_pair(1, more * PER_ROUND + LEAST * PER_ROUND)

            def store_step(b, first, count):
                act.wait_ge(f_out_set, count)
                act.dma_start(out[bass.ds(first, FC * CHUNK), :].rearrange("(c p r) d -> p c r d", p=P, c=FC),
                              fs[b][:]).then_inc(f_stored[b], 16)

            act.wait_ge(f_out_set, 1)
            act.dma_start(out[0:CHUNK, :].rearrange("(p r) d -> p r d", p=P), fs[0][:, 0]).then_inc(f_stored[0], 16)
            act.wait_ge(f_stored[0], 16)
            act.dma_start(out[CHUNK - OVER:2 * CHUNK - OVER, :].rearrange("(p r) d -> p r d", p=P), fs[0][:, 1]
                          ).then_inc(f_stored[0], 16)
            for t in range(1, FB):
                store_step(t, FC * t * CHUNK - OVER, t + 1)
            with act.Fori(1, STEPS // FB) as k:
                for b in range(FB):
                    store_step(b, k * (FC * FB * CHUNK) + (FC * b * CHUNK - OVER), k * FB + (b + 1))
            store_step(0, FC * STEPS * CHUNK - OVER, STEPS + 1)
            for b in range(FB):
                act.wait_ge(f_stored[b], 16 * (STEPS // FB + (2 if b == 0 else 0)))

        @block.vector
        def _(dve):
            count = [0]

            def step(ins):
                count[0] += 1
                ins.then_inc(setup, 1)
                dve.wait_ge(setup, count[0])

            for raw, what in ((s_raw, -2), (d_raw, -1), (d_next, FAR)):
                nc.vector.memset(raw[PAD_FROM:P, LAST - 1:COLS], what).then_inc(padded, 1)
            dve.wait_ge(lists_in, 16 * 6)
            step(nc.vector.tensor_tensor(loop_e[:], s_raw[:], d_raw[:], ALU.is_equal))
            dve.wait_ge(next_in, 16 * 3)
            step(nc.vector.tensor_tensor(drop[:], d_raw[:], d_next[:], ALU.not_equal))
            step(nc.vector.tensor_tensor(loop_e[:], loop_e[:], drop[:], ALU.mult))
            step(nc.vector.tensor_tensor(drop[:], d_raw[:], d_next[:], ALU.is_gt))
            step(nc.vector.tensor_reduce(counts[:, 0:1], loop_e[:], AX.X, ALU.add))
            step(nc.vector.tensor_reduce(counts[:, 1:2], drop[:], AX.X, ALU.add))
            assert count[0] == COUNTED
            step(nc.vector.tensor_tensor_scan(ahead_n[:], loop_e[:], loop_e[:], 0.0, ALU.add, ALU.max))
            dve.wait_ge(sums, 1)
            step(nc.vector.tensor_scalar(flags[:, 0:1], bank[7][:, 0:1], float(N), None, ALU.is_equal))
            step(nc.vector.tensor_scalar(flags[:, 1:2], bank[7][:, 1:2], 0.0, None, ALU.is_equal))
            step(nc.vector.scalar_tensor_tensor(out=flags[:, 2:3], in0=flags[:, 0:1], scalar=2.0,
                                                in1=flags[:, 1:2], op0=ALU.mult, op1=ALU.mult))
            step(nc.vector.tensor_scalar(flags[:, 3:4], flags[:, 2:3], -0.5, None, ALU.mult))
            step(nc.vector.tensor_scalar(flags[:, 4:5], flags[:, 2:3], 0.5, None, ALU.mult))
            step(nc.vector.scalar_tensor_tensor(out=kept[:], in0=counts[:, 0:1], scalar=flags[:, 3:4], in1=in_list[:],
                                                op0=ALU.mult, op1=ALU.add))
            step(nc.vector.tensor_scalar(tail_n[:], kept[:].to_broadcast([P, P]), float(-TAIL), 0.0, ALU.add, ALU.max))
            step(nc.vector.tensor_scalar(upto[:], before[:], -1.0, 1.0, ALU.mult, ALU.add))
            assert count[0] == KEPT
            step(nc.vector.tensor_scalar(drop[:], loop_e[:], flags[:, 3:4], flags[:, 4:5], ALU.mult, ALU.add))
            step(nc.vector.tensor_tensor(shift_i[:], ahead_n[:], drop[:], ALU.mult))
            step(nc.vector.scalar_tensor_tensor(out=packed[:, 0], in0=s_raw[:], scalar=BITS, in1=shift_i[:],
                                                op0=ALU.logical_shift_left, op1=ALU.bitwise_or))
            for b in range(BITS):
                old, new, far = packed[:, b % 2], packed[:, (b + 1) % 2], 1 << b
                step(nc.vector.tensor_scalar(moves[:], old, 31 - b, 31, ALU.logical_shift_left,
                                             ALU.arith_shift_right))
                step(nc.vector.scalar_tensor_tensor(out=new, in0=moves[:], scalar=-1, in1=old,
                                                    op0=ALU.bitwise_xor, op1=ALU.bitwise_and))
                step(nc.vector.copy_predicated(new[:, 0:COLS - far], moves[:, far:], old[:, far:]))
            step(nc.vector.tensor_scalar(shift_i[:], packed[:, BITS % 2], BITS, None, ALU.arith_shift_right))
            step(nc.vector.tensor_copy(edges[:, 0:COLS, 0], shift_i[:]))
            step(nc.vector.tensor_scalar(moves[:], packed[:, BITS % 2], (1 << BITS) - 1, None, ALU.bitwise_and))
            step(nc.vector.tensor_copy(d_first[:], d_raw[:, 0:1]))
            step(nc.vector.scalar_tensor_tensor(out=drop[:], in0=moves[:], scalar=d_first[:], in1=d_raw[:],
                                                op0=ALU.add, op1=ALU.subtract))
            step(nc.vector.scalar_tensor_tensor(out=edges[:, 0:COLS, 1], in0=drop[:], scalar=flags[:, 4:5],
                                                in1=d_raw[:], op0=ALU.mult, op1=ALU.add))
            step(nc.vector.tensor_copy(flat(edges[:, COLS:, :]), spare[:, 0:1].to_broadcast([P, (WIDE - COLS) * ENDS])))
            step(nc.vector.tensor_scalar(moves[:], column[:], kept[:, 0:1], None, ALU.is_ge))
            for e in range(ENDS):
                step(nc.vector.copy_predicated(edges[:, 0:COLS, e], moves[:], spare[:, 0:1].to_broadcast([P, COLS])))
            assert count[0] == LISTED
            tail_count = [0]

            def tail_step(ins):
                tail_count[0] += 1
                ins.then_inc(tail_steps, 1)
                dve.wait_ge(tail_steps, tail_count[0])

            dve.wait_ge(tail_summed, 1)
            tail_step(nc.vector.tensor_copy(tail_end[:], bank[5][:, 0:P]))
            tail_step(nc.vector.tensor_scalar(fits[:], tail_end[:, P - 1:P], float(SPREAD * P), None, ALU.is_le))
            dve.wait_ge(sums, 2)
            step(nc.vector.tensor_reduce(rounds_f[:, 0:1], bank[6][0:1, 0:P], AX.X, ALU.max))
            step(nc.vector.tensor_scalar(rounds_f[:, 1:2], rounds_f[:, 0:1], float(ROUND - 1 - LEAST * ROUND), 0.0,
                                         ALU.add, ALU.max))
            step(nc.vector.tensor_scalar(rounds_f[:, 0:1], fits[0:1, :], -1.0, 1.0, ALU.mult, ALU.add))
            step(nc.vector.tensor_tensor(rounds_i[:, 1:2], rounds_f[:, 1:2], rounds_f[:, 0:1], ALU.mult))
            nc.vector.tensor_scalar(rounds_i[:, 0:1], rounds_i[:, 1:2], ROUND.bit_length() - 1, None,
                                    ALU.arith_shift_right).then_inc(rounds_set, 1)
            dve.wait_ge(weights_in, ALL_WEIGHTS)
            step(nc.vector.tensor_tensor(w1s[:], w1[:], w1x[:], ALU.add))
            assert count[0] == SETUP_DONE

            def prepare(u, cols):
                nc.vector.tensor_scalar(g_idx[u][:], cols, float(N - 1), None, ALU.min).then_inc(g_idx_set, 1)

            def centre_pair(u, m, between=None):
                nc.vector.tensor_reduce(e_sum[:], rows[u][:], AX.X, ALU.add).then_inc(e_summed, 1)
                if between:
                    between()
                dve.wait_ge(e_summed, m)
                nc.vector.scalar_tensor_tensor(out=e_cen[:], in0=each(e_sum[:]), scalar=-1.0 / D, in1=rows[u][:],
                                               op0=ALU.mult, op1=ALU.add).then_inc(e_centred, 1)

            def var_pair(m):
                dve.wait_ge(e_squared, m)
                nc.vector.tensor_reduce(e_var[:], e_sq[:], AX.X, ALU.add).then_inc(e_var_set, 1)

            def node_pair(m):
                dve.wait_ge(e_std_set, m)
                nc.vector.reciprocal(e_inv[:], e_std[:]).then_inc(e_inv_set, 1)
                dve.wait_ge(e_inv_set, m)
                nc.vector.scalar_tensor_tensor(out=e_h[:], in0=e_cen[:], scalar=0.0, in1=each(e_inv[:]),
                                               op0=ALU.max, op1=ALU.mult).then_inc(e_h_set, 1)

            def aim_pair(v, m):
                dve.wait_ge(goal_set, m)
                dve.wait_ge(scattered, m)
                nc.vector.tensor_copy(s_idx[v][:], goal[v][:]).then_inc(s_idx_set, 1)

            def dve_slot(u, k, new, old, first=False, hold=False):
                n, m = k * 2 + (u + 1), k * 2 + (u + 2)

                def cross():
                    dve.wait_ge(ends_in[u], k * 16 + 16)
                    nc.vector.tensor_tensor(seen[u][:, :, 2], by_tile(ends[u])[:, :, 0],
                                            by_tile_column(k, u * TILES)[:, :, 1].unsqueeze(2).to_broadcast([P, TILES, P]),
                                            ALU.is_equal).then_inc(seen_set, 1)

                dve.wait_ge(gathered[1 - u], k * (16 * SLOTS) + 16 * SLOTS * (u + 1))
                centre_pair(1 - u, m, between=cross)
                prepare(1 - u, columns(k, (u + 3) * TILES))
                nc.vector.tensor_tensor(same[u][:], ends[u][:],
                                        columns(k, u * TILES).unsqueeze(2).to_broadcast([P, SLOTS, P]),
                                        ALU.is_equal).then_inc(same_set, 1)
                var_pair(m)
                dve.wait_ge(same_set, n)
                nc.vector.tensor_tensor(seen[u][:, :, 0:2], by_tile(same[u]),
                                        before[:].unsqueeze(1).unsqueeze(1).to_broadcast([P, TILES, ENDS, P]),
                                        ALU.mult).then_inc(seen_set, 1)
                dve.wait_ge(e_turned, n)
                node_pair(m)
                dve.wait_ge(seen_set, k * 4 + (2 * u + 2))
                nc.vector.tensor_reduce(by_end(dup, 1), seen[u][:, :, 1:3].rearrange("p t c q -> p t (c q)"), AX.X,
                                        ALU.add).then_inc(dup_set, 1)
                nc.vector.tensor_reduce(by_end(dup, 0), seen[u][:, :, 0], AX.X, ALU.add).then_inc(dup_set, 1)
                if not first:
                    aim_pair(1 - u, k * 2 + u)
                if new and u == 0:
                    dve.wait_ge(n_in, k * 16 + 16)
                    nc.vector.tensor_reduce(n_sum[:], nx[:], AX.X, ALU.add).then_inc(n_summed, 1)
                dve.wait_ge(dup_set, k * 4 + (2 * u + 2))
                nc.vector.scalar_tensor_tensor(out=away[:], in0=dup[:], scalar=0.0, in1=spare[:],
                                               op0=ALU.is_gt, op1=ALU.mult).then_inc(away_set, 1)
                if new and u == 0:
                    dve.wait_ge(n_summed, k + 1)
                    nc.vector.scalar_tensor_tensor(out=n_cen[:], in0=each(n_sum[:]), scalar=-1.0 / D, in1=nx[:],
                                                   op0=ALU.mult, op1=ALU.add).then_inc(n_centred, 1)
                if old and u == 1:
                    dve.wait_ge(n_msg_made, k)
                    if hold:
                        to = held_chunks(k - 1, 1)[:, 0]
                    else:
                        dve.wait_ge(n_out_free, k - HELD)
                        to = n_out[:]
                    nc.vector.scalar_tensor_tensor(out=to, in0=N_MSG[:].rearrange("p (r d) -> p r d", r=R),
                                                   scalar=flags[:, 2:3], in1=n_xh[:], op0=ALU.mult,
                                                   op1=ALU.add).then_inc(n_out_set, 1)
                if new and u == 0:
                    dve.wait_ge(n_squared, k + 1)
                    nc.vector.tensor_reduce(n_var[:], n_sq[:], AX.X, ALU.add).then_inc(n_var_set, 1)
                dve.wait_ge(e_msg_made, n)
                dve.wait_ge(e_part_set, k * 4 + (2 * u + 1))
                nc.vector.tensor_tensor(e_rest[:], messages(), e_part[:, 0], ALU.subtract).then_inc(e_rest_set, 1)
                if new and u == 0:
                    dve.wait_ge(n_std_set, k + 1)
                    nc.vector.reciprocal(n_inv[:], n_std[:]).then_inc(n_inv_set, 1)
                    dve.wait_ge(n_inv_set, k + 1)
                    nc.vector.scalar_tensor_tensor(out=n_h[:], in0=n_cen[:], scalar=0.0, in1=each(n_inv[:]),
                                                   op0=ALU.max, op1=ALU.mult).then_inc(n_h_set, 1)
                if new and u == 1:
                    dve.wait_ge(n_h_set, k + 1)
                    if old:
                        dve.wait_ge(n_out_set, k)
                    nc.vector.tensor_tensor(n_xh[:], nx[:], n_h[:], ALU.add).then_inc(n_xh_set, 1)
                dve.wait_ge(e_rest_set, n)
                dve.wait_ge(e_part_set, k * 4 + (2 * u + 2))
                nc.vector.tensor_tensor(e_part[:, 2], e_rest[:], e_part[:, 1], ALU.subtract).then_inc(e_split_set, 1)
                dve.wait_ge(away_set, n)
                nc.vector.tensor_tensor(goal[u][:], columns(k, u * TILES), away[:], ALU.max).then_inc(goal_set, 1)

            def deal_tail():
                tail_step(nc.vector.tensor_tensor(ended[:], tail_end[:].unsqueeze(1).to_broadcast([P, SPREAD, P]),
                                                  rank[:].unsqueeze(2).to_broadcast([P, SPREAD, P]), ALU.is_le))
                tail_step(nc.vector.tensor_reduce(whose[:], ended[:], AX.X, ALU.add))
                tail_step(nc.vector.tensor_tensor(ended_at[:], tail_end[:].unsqueeze(1).to_broadcast([P, SPREAD, P]),
                                                  ended[:], ALU.mult))
                tail_step(nc.vector.tensor_reduce(its_first[:], ended_at[:], AX.X, ALU.max))
                tail_step(nc.vector.scalar_tensor_tensor(out=row[:], in0=whose[:], scalar=float(TAIL_W), in1=rank[:],
                                                         op0=ALU.mult, op1=ALU.add))
                tail_step(nc.vector.tensor_tensor(row[:], row[:], its_first[:], ALU.subtract))
                tail_step(nc.vector.tensor_scalar(row_is[:], rank[:], tail_end[:, P - 1:P], None, ALU.is_lt))
                tail_step(nc.vector.scalar_tensor_tensor(out=row[:], in0=row[:], scalar=none[:], in1=row_is[:],
                                                         op0=ALU.subtract, op1=ALU.mult))
                tail_step(nc.vector.tensor_scalar(row[:], row[:], none[:], None, ALU.add))
                tail_step(nc.vector.tensor_tensor(row[:], row[:], stay[:], ALU.subtract))
                tail_step(nc.vector.scalar_tensor_tensor(out=row[:], in0=row[:], scalar=fits[:], in1=stay[:],
                                                         op0=ALU.mult, op1=ALU.add))
                nc.vector.tensor_copy(row_i[:], row[:]).then_inc(tail_idx_set, 1)

            def part_b2():
                done = [0]

                def b2_step(ins):
                    done[0] += 1
                    ins.then_inc(b2_steps, 1)
                    dve.wait_ge(b2_steps, done[0])

                b2_step(nc.vector.tensor_copy(ones_b[:], ones[:]))
                b2_step(nc.vector.tensor_copy(b2_part[:, 0], b2r[:]))
                b2_step(nc.vector.tensor_tensor(b2_rest[:], b2r[:], b2_part[:, 0], ALU.subtract))
                b2_step(nc.vector.tensor_copy(b2_part[:, 1], b2_rest[:]))
                b2_step(nc.vector.tensor_tensor(b2_part[:, 2], b2_rest[:], b2_part[:, 1], ALU.subtract))
                b2_step(nc.vector.tensor_scalar(b2_own[:], b2_part[:, 0], ident[:, 0:1], None, ALU.mult))
                for part in range(1, PARTS):
                    b2_step(nc.vector.scalar_tensor_tensor(out=b2_own[:], in0=b2_part[:, part],
                                                           scalar=ident[:, part:part + 1], in1=b2_own[:],
                                                           op0=ALU.mult, op1=ALU.add))
                b2_step(nc.vector.tensor_copy(b2s[:], b2_own[:].unsqueeze(1).to_broadcast([P, R, D])))
                assert done[0] == B2_DONE

            more = more_rounds(dve)
            for i in range(3):
                if i == 2:
                    deal_tail()
                    part_b2()
                    dve.wait_ge(gathered[0], 16 * SLOTS)
                    centre_pair(0, 1)
                prepare(i % 2, flat(edges[:, i * TILES:(i + 1) * TILES, :]))
            var_pair(1)
            node_pair(1)
            for u in range(2):
                dve_slot(u, 0, True, False, first=(u == 0))
            dve.wait_ge(tail_in, 16 * SPREAD)
            dve.wait_ge(filled, 16 * N_FILLS)
            with dve.Fori(1, HELD + 1) as k:
                for u in range(2):
                    dve_slot(u, k, True, True, hold=True)
            with dve.Fori(HELD + 1, NCH) as k:
                for u in range(2):
                    dve_slot(u, k, True, True)
            for u in range(2):
                dve_slot(u, NCH, False, True)
            with dve.Fori(NCH + 1, more + LEAST) as k:
                for u in range(2):
                    dve_slot(u, k, False, False)
            aim_pair(1, more * PER_ROUND + LEAST * PER_ROUND)

            def sum_step(b, landed, more_of_it):
                dve.wait_ge(f_in[b], landed)
                nc.vector.tensor_tensor(fs[b][:], fs[b][:], more_of_it, ALU.add).then_inc(f_out_set, 1)

            for t in range(FB):
                sum_step(t, 32 if t == 0 else 16, held_chunks(t * FC, FC))
            with dve.Fori(1, HELD_TURNS) as k:
                for b in range(FB):
                    sum_step(b, k * 16 + (32 if b == 0 else 16), held_chunks(k * (FC * FB) + b * FC, FC))
            with dve.Fori(HELD_TURNS, STEPS // FB) as k:
                for b in range(FB):
                    sum_step(b, k * 32 + ((48 if b == 0 else 32) - 16 * HELD_TURNS), fn[b][:])
            sum_step(0, 32 * (STEPS // FB) + (48 - 16 * HELD_TURNS), fn[0][:])

        @block.tensor
        def _(pe):
            pe.wait_ge(consts, ALL_CONSTS)
            pe.wait_ge(setup, COUNTED)
            nc.tensor.matmul(bank[7][:, 0:2], ones[:], counts[:], start=True, stop=True).then_inc(sums, 1)
            pe.wait_ge(setup, KEPT)
            nc.tensor.transpose(bank[6][0:1, 0:P], kept[:], ident[:]).then_inc(sums, 1)
            nc.tensor.matmul(bank[5][:, 0:P], tail_n[:], upto[:], start=True, stop=True).then_inc(tail_summed, 1)
            pe.wait_ge(setup, LISTED)
            for n, group in enumerate(GROUPS):
                for b in group:
                    last = nc.tensor.transpose(bank[n][:, (b % 4) * P:(b % 4 + 1) * P],
                                               flat(edges[:, b * P // ENDS:(b + 1) * P // ENDS, :]), ident[:])
                last.then_inc(list_turned, 1)
            pe.wait_ge(weights_in, ALL_WEIGHTS)
            pe.wait_ge(setup, SETUP_DONE)
            pe.wait_ge(list_copied, len(GROUPS))

            def turn_pair(m):
                pe.wait_ge(e_h_set, m)
                for t in range(TILES):
                    last = nc.tensor.transpose(E_TURN[:, t * P:(t + 1) * P],
                                               flat(e_h[:, ENDS * t:ENDS * (t + 1), :]), ident[:])
                last.then_inc(e_turned, 1)

            def turn_chunk(k):
                pe.wait_ge(n_h_set, k + 1)
                for r in range(R // 2):
                    last = nc.tensor.transpose(N_TURN[:, r * P:(r + 1) * P], flat(n_h[:, 2 * r:2 * r + 2, :]), ident[:])
                last.then_inc(n_turned, 1)

            def hidden_chunk(k):
                pe.wait_ge(n_hT_set, k + 1)
                for half in range(2):
                    part = slice(half * D, half * D + D)
                    nc.tensor.matmul(N_HID[half][:], w1s[part, :], n_hT[part, :], start=True, stop=True
                                     ).then_inc(n_hid_made, 1)

            def message_chunk(k, half):
                if half == 0:
                    nc.tensor.matmul(N_MSG[:], ones_b[0:PARTS, :], flat(b2s[0:PARTS]), start=True, stop=False)
                pe.wait_ge(n_hid_set, k * 2 + (half - 1))
                for r in range(R // 2):
                    o = (2 * r + half) * D
                    last = nc.tensor.matmul(N_MSG[:, o:o + D], n_hid[:, half, r * P:(r + 1) * P], w2[:],
                                            start=False, stop=(half == 1 and r == R // 2 - 1))
                if half == 1:
                    last.then_inc(n_msg_made, 1)

            def sum_pair(v, n):
                pe.wait_ge(e_split_set, n)
                pe.wait_ge(same_set, n)
                pe.wait_ge(seen_set, n * 2)
                for t in range(TILES):
                    src_s, dst_s = ENDS * t, ENDS * t + 1
                    for s, terms in ((src_s, ((same[v][:, src_s, :], src_s), (seen[v][:, t, 2, :], dst_s))),
                                     (dst_s, ((same[v][:, dst_s, :], dst_s),))):
                        for i, (shares, whose) in enumerate(terms):
                            for part in range(PARTS):
                                last = nc.tensor.matmul(E_UPD[:, s * D:(s + 1) * D], shares, e_part[:, part, whose, :],
                                                        start=(i == 0 and part == 0),
                                                        stop=(i == len(terms) - 1 and part == PARTS - 1))
                last.then_inc(e_upd_made, 1)

            def pe_slot(u, k, new, old, first=False):
                n, m = k * 2 + (u + 1), k * 2 + (u + 2)
                pe.wait_ge(e_hT_set, n)
                for end, w in enumerate((w1, w1x)):
                    last = nc.tensor.matmul(E_HID[:, end * TILES * P:(end + 1) * TILES * P], w[:], e_hT[:],
                                            start=True, stop=True)
                last.then_inc(e_hid_made, 1)
                if not first:
                    sum_pair(1 - u, k * 2 + u)
                if new and u == 1:
                    turn_chunk(k)
                turn_pair(m)
                if first:
                    pe.wait_ge(b2_steps, B2_DONE)
                nc.tensor.matmul(E_MSG[:, 0:SLOTS * D], ones_b[0:PARTS, :], flat(b2s[0:PARTS, 0:SLOTS]), start=True, stop=False)
                pe.wait_ge(e_hid_set, n)
                for t in range(TILES):
                    for end in range(ENDS):
                        s = ENDS * t + end
                        last = nc.tensor.matmul(E_MSG[:, s * D:(s + 1) * D], e_hid[:, end, t, :], w2[:],
                                                start=False, stop=(s == SLOTS - 1))
                last.then_inc(e_msg_made, 1)
                if old and u == 0:
                    message_chunk(k, 0)
                if old and u == 0:
                    message_chunk(k, 1)
                if new and u == 1:
                    hidden_chunk(k)

            more = more_rounds(pe)
            turn_pair(1)
            for u in range(2):
                pe_slot(u, 0, True, False, first=(u == 0))
            pe.wait_ge(tail_in, 16 * SPREAD)
            pe.wait_ge(e_hT_set, PER_ROUND + 1)
            nc.tensor.transpose(E_TURN[:, TILES * P:(TILES + 1) * P],
                                flat(edges[:, TAIL_BLOCK * P // ENDS:(TAIL_BLOCK + 1) * P // ENDS, :]), ident[:]
                                ).then_inc(tail_turned, 1)
            pe.wait_ge(tail_copied, 1)
            with pe.Fori(1, NCH) as k:
                for u in range(2):
                    pe_slot(u, k, True, True)
            for u in range(2):
                pe_slot(u, NCH, False, True)
            with pe.Fori(NCH + 1, more + LEAST) as k:
                for u in range(2):
                    pe_slot(u, k, False, False)
            sum_pair(1, more * PER_ROUND + LEAST * PER_ROUND)


_INS = ["x", "src", "dst", "L0_gnn_W1", "L0_gnn_b1", "L0_gnn_W2", "L0_gnn_b2"]


def kernel(**inputs):
    import numpy as _np
    import concourse.bacc as _bacc
    from concourse import mybir as _mybir
    from concourse.bass_utils import run_bass_kernel_spmd as _run

    nc = _bacc.Bacc("TRN2", target_bir_lowering=False, num_devices=1)
    arrays, args = {}, []
    for name in _INS:
        a = _np.ascontiguousarray(inputs[name])
        arrays[f"in_{name}_dram"] = a
        args.append(nc.dram_tensor(f"in_{name}_dram", a.shape, _mybir.dt.from_np(a.dtype), kind="ExternalInput").ap())
    out = nc.dram_tensor("out_dram", arrays["in_x_dram"].shape, _mybir.dt.float32, kind="ExternalOutput").ap()
    gnn_layer(nc, *args, out)
    r = _run(nc, [arrays], core_ids=[0])
    return r.results[0]["out_dram"]
```
